# Optimizing a Trainium2 kernel written in Bass

```python
import numpy as np
import jax
import jax.numpy as jnp

def _softmax(x, axis=-1):
    return jax.nn.softmax(x, axis=axis)

def _gelu(x):
    return jax.nn.gelu(x, approximate=True)

def _silu(x):
    return jax.nn.silu(x)

def _sigmoid(x):
    return jax.nn.sigmoid(x)

def _layernorm(x, axis=-1, eps=1e-05):
    m = jnp.mean(x, axis=axis, keepdims=True)
    v = jnp.var(x, axis=axis, keepdims=True)
    return (x - m) / jnp.sqrt(v + eps)

def _scatter_add(tgt, idx, src, axis=0):
    return tgt.at[idx].add(src)

def _segment_sum(src, seg, n):
    return jax.ops.segment_sum(src, seg, n)
kernel_name = 'mk_adj_resnorm_d2_adj_r2_614392'

def setup_inputs(seed: int=0):
    np.random.seed(seed)
    _w = jnp.asarray

    def _rec_inputs():
        import jax
        import jax.numpy as jnp
        _gk = jax.random.key(seed)
        x = -0.0001538 + 1 * jax.random.normal(jax.random.fold_in(_gk, 1), (32, 256, 384), jnp.float32)
        _w = (1.0 + jnp.arange(256, dtype=jnp.float32)) ** (-0.5)
        _w = _w / _w.mean()
        _pij = jnp.clip(0.0625 * _w[:, None] * _w[None, :], 0.0, 1.0)
        _a = jax.random.uniform(jax.random.fold_in(_gk, 2), (32, 256, 256)) < _pij
        _af = _a.astype(jnp.float32)
        adj = _af
        return (x, adj)
    x, adj = _rec_inputs()

    def _L0_gnn_setup():
        import jax, jax.numpy as jnp
        import numpy as np
        LN_EPS = 1e-12

        def _digcn_forward(hidden_state, adjacency_matrix, Wl, bl, Ws, bs, Wr, br, ln_w, ln_b):
            B, S, D = hidden_state.shape
            temper = jnp.asarray(D, jnp.float32) ** 0.5
            i = jnp.arange(S)
            upper = (i[None, :] > i[:, None]).astype(hidden_state.dtype)
            lower = (i[None, :] < i[:, None]).astype(hidden_state.dtype)

            def layer(h, params):
                wl, b_l, ws, b_s, wr, b_r, g, beta = params
                u = jnp.einsum('bid,bjd->bij', h, h) / temper
                a = jax.nn.softmax(u, axis=-1)
                delta = a * adjacency_matrix
                attn = delta / (jnp.sum(delta, axis=-1, keepdims=True) + 1e-10)
                hl = h @ wl.T + b_l
                hs = h @ ws.T + b_s
                hr = h @ wr.T + b_r
                diag_a = jnp.diagonal(attn, axis1=1, axis2=2)
                ctx = jnp.einsum('bij,bjd->bid', attn * upper, hl) + diag_a[..., None] * hs + jnp.einsum('bij,bjd->bid', attn * lower, hr)
                mean = ctx.mean(-1, keepdims=True)
                var = ctx.var(-1, keepdims=True)
                o = (ctx - mean) / jnp.sqrt(var + LN_EPS) * g + beta
                return (jax.nn.relu(o), None)
            out, _ = jax.lax.scan(layer, hidden_state, (Wl, bl, Ws, bs, Wr, br, ln_w, ln_b))
            return out
        key = jax.random.key(seed)
        ks = jax.random.split(key, 6)
        B, S, D, L = (8, 512, 384, 2)
        scale = (1.0 / D) ** 0.5
        hidden_state = jax.random.normal(ks[0], (B, S, D), jnp.float32)
        adjacency_matrix = (jax.random.uniform(ks[1], (B, S, S)) < 0.05).astype(jnp.float32)
        Wl = jax.random.normal(ks[2], (L, D, D), jnp.float32) * scale
        Ws = jax.random.normal(ks[3], (L, D, D), jnp.float32) * scale
        Wr = jax.random.normal(ks[4], (L, D, D), jnp.float32) * scale
        bl = jnp.zeros((L, D), jnp.float32)
        bs = jnp.zeros((L, D), jnp.float32)
        br = jnp.zeros((L, D), jnp.float32)
        ln_w = jnp.ones((L, D), jnp.float32)
        ln_b = jnp.zeros((L, D), jnp.float32)
        return dict(hidden_state=hidden_state, adjacency_matrix=adjacency_matrix, Wl=Wl, bl=bl, Ws=Ws, bs=bs, Wr=Wr, br=br, ln_w=ln_w, ln_b=ln_b)
    _L0_gnn_all = _L0_gnn_setup()
    _L0_gnn_in = {k: v for k, v in _L0_gnn_all.items() if k in ('Wl', 'bl', 'Ws', 'bs', 'Wr', 'br', 'ln_w', 'ln_b')}
    del _L0_gnn_all

    def _L1_gnn_setup():
        import jax, jax.numpy as jnp
        import numpy as np
        B, N, D, H = (8, 512, 384, 12)
        HD = D // H

        def _split_heads(x):
            b, n, _ = x.shape
            return x.reshape(b, n, H, HD).transpose(0, 2, 1, 3)
        key = jax.random.key(seed)
        ks = jax.random.split(key, 10)
        input_graph = jax.random.normal(ks[0], (B, N, D), dtype=jnp.float32)
        u = jax.random.uniform(ks[1], (B, N, N), dtype=jnp.float32)
        keep = jax.random.uniform(ks[2], (B, N, N)) < 0.15
        adj = jnp.where(keep, u, 0.0)
        s = 1.0 / np.sqrt(D)
        Wq = jax.random.normal(ks[3], (D, D), dtype=jnp.float32) * s
        bq = jnp.zeros((D,), dtype=jnp.float32)
        Wk = jax.random.normal(ks[4], (D, D), dtype=jnp.float32) * s
        bk = jnp.zeros((D,), dtype=jnp.float32)
        Wv = jax.random.normal(ks[5], (D, D), dtype=jnp.float32) * s
        bv = jnp.zeros((D,), dtype=jnp.float32)
        beta = jnp.asarray(0.1, dtype=jnp.float32)
        return {'input_graph': input_graph, 'adj': adj, 'Wq': Wq, 'bq': bq, 'Wk': Wk, 'bk': bk, 'Wv': Wv, 'bv': bv, 'beta': beta}
    _L1_gnn_all = _L1_gnn_setup()
    _L1_gnn_in = {k: v for k, v in _L1_gnn_all.items() if k in ('Wq', 'bq', 'Wk', 'bk', 'Wv', 'bv', 'beta')}
    del _L1_gnn_all
    return {'x': x, 'adj': adj, 'L0_gnn_Wl': _L0_gnn_in['Wl'], 'L0_gnn_bl': _L0_gnn_in['bl'], 'L0_gnn_Ws': _L0_gnn_in['Ws'], 'L0_gnn_bs': _L0_gnn_in['bs'], 'L0_gnn_Wr': _L0_gnn_in['Wr'], 'L0_gnn_br': _L0_gnn_in['br'], 'L0_gnn_ln_w': _L0_gnn_in['ln_w'], 'L0_gnn_ln_b': _L0_gnn_in['ln_b'], 'L1_gnn_Wq': _L1_gnn_in['Wq'], 'L1_gnn_bq': _L1_gnn_in['bq'], 'L1_gnn_Wk': _L1_gnn_in['Wk'], 'L1_gnn_bk': _L1_gnn_in['bk'], 'L1_gnn_Wv': _L1_gnn_in['Wv'], 'L1_gnn_bv': _L1_gnn_in['bv'], 'L1_gnn_beta': _L1_gnn_in['beta']}

def reference(x, adj, L0_gnn_Wl, L0_gnn_bl, L0_gnn_Ws, L0_gnn_bs, L0_gnn_Wr, L0_gnn_br, L0_gnn_ln_w, L0_gnn_ln_b, L1_gnn_Wq, L1_gnn_bq, L1_gnn_Wk, L1_gnn_bk, L1_gnn_Wv, L1_gnn_bv, L1_gnn_beta):
    import jax
    import jax.numpy as jnp

    def _L0_gnn_ref(hidden_state, adjacency_matrix, Wl, bl, Ws, bs, Wr, br, ln_w, ln_b):
        import jax, jax.numpy as jnp
        import numpy as np
        LN_EPS = 1e-12

        def _digcn_forward(hidden_state, adjacency_matrix, Wl, bl, Ws, bs, Wr, br, ln_w, ln_b):
            B, S, D = hidden_state.shape
            temper = jnp.asarray(D, jnp.float32) ** 0.5
            i = jnp.arange(S)
            upper = (i[None, :] > i[:, None]).astype(hidden_state.dtype)
            lower = (i[None, :] < i[:, None]).astype(hidden_state.dtype)

            def layer(h, params):
                wl, b_l, ws, b_s, wr, b_r, g, beta = params
                u = jnp.einsum('bid,bjd->bij', h, h) / temper
                a = jax.nn.softmax(u, axis=-1)
                delta = a * adjacency_matrix
                attn = delta / (jnp.sum(delta, axis=-1, keepdims=True) + 1e-10)
                hl = h @ wl.T + b_l
                hs = h @ ws.T + b_s
                hr = h @ wr.T + b_r
                diag_a = jnp.diagonal(attn, axis1=1, axis2=2)
                ctx = jnp.einsum('bij,bjd->bid', attn * upper, hl) + diag_a[..., None] * hs + jnp.einsum('bij,bjd->bid', attn * lower, hr)
                mean = ctx.mean(-1, keepdims=True)
                var = ctx.var(-1, keepdims=True)
                o = (ctx - mean) / jnp.sqrt(var + LN_EPS) * g + beta
                return (jax.nn.relu(o), None)
            out, _ = jax.lax.scan(layer, hidden_state, (Wl, bl, Ws, bs, Wr, br, ln_w, ln_b))
            return out
        return _digcn_forward(hidden_state, adjacency_matrix, Wl, bl, Ws, bs, Wr, br, ln_w, ln_b)

    def _L1_gnn_ref(input_graph, adj, Wq, bq, Wk, bk, Wv, bv, beta):
        import jax, jax.numpy as jnp
        import numpy as np
        B, N, D, H = (8, 512, 384, 12)
        HD = D // H

        def _split_heads(x):
            b, n, _ = x.shape
            return x.reshape(b, n, H, HD).transpose(0, 2, 1, 3)
        q = _split_heads(input_graph @ Wq + bq)
        k = _split_heads(input_graph @ Wk + bk)
        v = _split_heads(input_graph @ Wv + bv)
        scores = jnp.einsum('bhqd,bhkd->bhqk', q, k) / jnp.sqrt(jnp.asarray(HD, input_graph.dtype))
        adj_e = adj[:, None, :, :]
        scores = scores + beta * adj_e
        scores = jnp.where(adj_e > 0, scores, jnp.asarray(-9000000000000000.0, scores.dtype))
        probs = jax.nn.softmax(scores, axis=-1)
        out = jnp.einsum('bhqk,bhkd->bhqd', probs, v)
        return out.transpose(0, 2, 1, 3).reshape(input_graph.shape[0], input_graph.shape[1], D)
    x = _layernorm(x + _L0_gnn_ref(x, adj, L0_gnn_Wl, L0_gnn_bl, L0_gnn_Ws, L0_gnn_bs, L0_gnn_Wr, L0_gnn_br, L0_gnn_ln_w, L0_gnn_ln_b), axis=-1)
    x = _layernorm(x + _L1_gnn_ref(x, adj, L1_gnn_Wq, L1_gnn_bq, L1_gnn_Wk, L1_gnn_bk, L1_gnn_Wv, L1_gnn_bv, L1_gnn_beta), axis=-1)
    return x

_drawn_inputs = setup_inputs


def setup_inputs(seed=0):
    import zlib

    import numpy as np

    out = dict(_drawn_inputs(seed))
    spreads = {'L0_gnn_bl': (0.0, 0.1),
     'L0_gnn_bs': (0.0, 0.1),
     'L0_gnn_br': (0.0, 0.1),
     'L0_gnn_ln_w': (1.0, 0.2),
     'L0_gnn_ln_b': (0.0, 0.1),
     'L1_gnn_bq': (0.0, 0.319),
     'L1_gnn_bk': (0.0, 0.8),
     'L1_gnn_bv': (0.0, 0.1)}
    factors = {}
    for name, (base, spread) in spreads.items():
        noise = np.random.default_rng([zlib.crc32(name.encode()), seed]).standard_normal(out[name].shape)
        drawn = base * np.exp(spread * noise) if base else spread * noise
        out[name] = jnp.asarray(drawn.astype(out[name].dtype))
    for name, factor in factors.items():
        out[name] = (out[name] * factor).astype(out[name].dtype)
    return out
```

```python
from contextlib import ExitStack

import numpy as np

import concourse.bass as bass
from concourse import mybir

F32 = mybir.dt.float32
F32R = mybir.dt.float32r
BF16 = mybir.dt.bfloat16
F16 = mybir.dt.float16
ALU = mybir.AluOpType
ACT = mybir.ActivationFunctionType
AX = mybir.AxisListType

P = 128
NH = 12
VP = 3
SLOTS = 3
RING = 3
EPS_GRAPH = 1e-12
EPS_NORM = 1e-5
EPS_ATTN = 1e-10
MASKED = -9000000000000000.0
BIG = 3.0e38
PARTS = ((0, 0), (0, 1), (1, 0))


def schedule(a, b, c):
    steps = []
    heads = list(range(NH + 2)) if c else []

    def head():
        if heads:
            k = heads.pop(0)
            if k < NH:
                steps.append(("scores", k))
            if 0 <= k - 1 < NH:
                steps.append(("weights", k - 1))
            if 0 <= k - 2 < NH:
                steps.append(("attend", k - 2))

    def add(on, *names):
        if on:
            steps.extend(names)

    add(c, *[("qk", j) for j in range(6)])
    add(c, ("v", 0), ("v", 1))
    add(b, *[("turn_h", k) for k in range(3)])
    add(b, ("b_scores", 0), ("b_proj", 0), ("b_proj", 1))
    head()
    add(b, ("b_proj", 2))
    head()
    add(b, ("b_proj", 3))
    head()
    add(b, ("b_turn", 0), ("b_proj", 4))
    head()
    add(b, ("b_proj", 5))
    add(a, ("turn_x", 0), ("turn_x", 1), ("turn_x", 2))
    head()
    add(a, ("a_scores", 0))
    add(b, ("b_mix", 0))
    head()
    add(b, ("b_mix", 1), ("b_norm", 0))
    add(a, ("a_proj", 0))
    head()
    add(a, ("a_proj", 1))
    add(b, ("b_norm2", 0))
    head()
    add(a, ("a_proj", 2))
    head()
    add(a, ("a_turn", 0), ("a_proj", 3))
    head()
    add(a, ("a_proj", 4))
    head()
    add(a, ("a_proj", 5))
    head()
    add(b, *[("turn_y", k) for k in range(3)])
    add(a, ("a_mix", 0))
    head()
    add(a, ("a_mix", 1), ("a_norm", 0))
    while heads:
        head()
    add(c, ("final", 0))
    return steps


def graph_attention_kernel(nc, x, adj, wl, ws, wr, bl, bs, br, ln_w, ln_b,
                           wq, wk, wv, bq, bk, bv, beta, out):
    NB, S, D = x.shape
    NT = S // P
    NC = D // P
    HD = D // NH
    HPG = P // HD
    LAYERS = wl.shape[0]
    TEMPER = float(D) ** -0.5
    SCALE = float(HD) ** -0.5
    assert NT == 2 and NC == 3 and LAYERS == 2 and HD == 32

    x_v = x.rearrange("b (i p) d -> b p i d", p=P)
    adj_v = adj.rearrange("b (i p) j -> b p i j", p=P)
    out_v = out.rearrange("b (i p) d -> b p i d", p=P)

    with ExitStack() as ctx:
        def sb(name, shape, dt=F32):
            return ctx.enter_context(nc.sbuf_tensor(name, shape, dt))

        def bank(name):
            return ctx.enter_context(nc.psum_tensor(name, [P, 512], F32))

        def sem(name):
            return ctx.enter_context(nc.semaphore(name))

        w_graph = [[sb(f"w_graph{l}{p}", [P, NC, 3, D], F32R) for p in "hl"] for l in range(LAYERS)]
        w_qkv = [sb(f"w_qkv{p}", [P, NC, 3, D], F32R) for p in "hl"]
        bias_rows = sb("bias_rows", [P, 3, D], F32R)
        pick_bias = [sb(f"pick_bias{l}", [P, P], F32R) for l in range(LAYERS)]
        ident = sb("ident", [P, P])
        mask_up = sb("mask_up", [P, P])
        mask_low = sb("mask_low", [P, P])
        q_bias = sb("q_bias", [P, NC])
        k_bias = sb("k_bias", [P, NC])
        v_bias = sb("v_bias", [P, D])
        g1_col = sb("g1_col", [P, NC])
        b1_col = sb("b1_col", [P, NC])
        g2_row = sb("g2_row", [P, D])
        b2_row = sb("b2_row", [P, D])
        beta_col = sb("beta_col", [P, 1])
        x_in = sb("x_in", [P, NT, D])
        adj_in = sb("adj_in", [P, NT, S])
        hT_ac = [sb(f"hT_ac{p}", [P, NC, S], F32R) for p in "hl"]
        hT_b = [sb(f"hT_b{p}", [P, NC, S], F32R) for p in "hl"]
        expu = sb("expu", [P, NT, S])
        attT = [sb(f"attT{p}", [P, NT, S], F32R) for p in "hl"]
        up = [sb(f"up{p}", [P, NT, P], F32R) for p in "hl"]
        low = [sb(f"low{p}", [P, NT, P], F32R) for p in "hl"]
        hlr = [sb(f"hlr{p}", [P, NT, 2, D], F32R) for p in "hl"]
        self_part = sb("self_part", [P, NT, D])
        mixed = sb("mixed", [P, NT, D])
        normed = sb("normed", [P, NT, D])
        diag_tmp = sb("diag_tmp", [P, P])
        y_in = sb("y_in", [P, NT, D])
        res = sb("res", [P, NT, D])
        bias_adj = sb("bias_adj", [P, NT, S])
        neg_adj = sb("neg_adj", [P, NT, S])
        qk_hi = sb("qk_hi", [P, RING, S], F32R)
        qk_lo = sb("qk_lo", [P, RING, S], F32R)
        q_st = sb("q_st", [P, NH, S], F32R)
        k_st = sb("k_st", [P, NH, S], F32R)
        v_parts = sb("v_parts", [P, NT, NH, VP, HD], BF16)
        v_rest = sb("v_rest", [P, NT, D])
        masked = sb("masked", [P, NT, S])
        prob = sb("prob", [P, 2, NT, S])
        pT_hi = sb("pT_hi", [P, 2, NT, S], F16)
        pT_lo = sb("pT_lo", [P, 2, NT, S], F16)
        att = sb("att", [P, NT, NH, HD])
        result = sb("result", [P, NT, D])
        negmax = sb("negmax", [P, NT])
        ubias = sb("ubias", [P, NT])
        zsum = sb("zsum", [P, NT])
        ssum = sb("ssum", [P, NT])
        diag = sb("diag", [P, NT])
        inv_s = sb("inv_s", [P, NT])
        hmin = sb("hmin", [P, NT, NH])
        hsum = sb("hsum", [P, NT, NH])
        hinv = sb("hinv", [P, NT, NH])
        stats = sb("stats", [P, NT, 6])
        mv = sb("mv", [P, NT, 2])
        var = sb("var", [P, NT])
        lnv = sb("lnv", [P, NT])
        y0 = sb("y0", [P, NT])
        tmp = sb("tmp", [P, NT])
        rstd = sb("rstd", [P, NT])

        staging = [buf[:, i, :] for buf in (normed, y_in, res, result, v_rest) for i in range(NT)][:9]

        bank_w = [bank("bank_w0"), bank("bank_w1")]
        bank_u = bank("bank_u")
        bank_t = bank("bank_t")
        bank_m = bank("bank_m")
        bank_s = bank("bank_s")
        bank_p = bank("bank_p")
        bank_o = bank("bank_o")

        s_setup = sem("s_setup")
        s_const = sem("s_const")
        s_stage = sem("s_stage")
        s_split = sem("s_split")
        s_pool_c = sem("s_pool_c")
        s_xa, s_xb = sem("s_xa"), sem("s_xb")
        s_adj = {k: sem(f"s_adj_{k}") for k in "abc"}
        s_tx_pe, s_tx_hi, s_tx_lo = sem("s_tx_pe"), sem("s_tx_hi"), sem("s_tx_lo")
        s_th_pe, s_th_f, s_th_lo = sem("s_th_pe"), sem("s_th_f"), sem("s_th_lo")
        s_ty_pe, s_ty_hi, s_ty_lo = sem("s_ty_pe"), sem("s_ty_hi"), sem("s_ty_lo")
        s_u, s_ub, s_exp, s_em = sem("s_u"), sem("s_ub"), sem("s_exp"), sem("s_em")
        s_proj, s_proj_hi, s_proj_rd = sem("s_proj"), sem("s_proj_hi"), sem("s_proj_rd")
        s_at, s_at_hi, s_at_lo, s_cut = sem("s_at"), sem("s_at_hi"), sem("s_at_lo"), sem("s_cut")
        s_mix, s_mix_rd = sem("s_mix"), sem("s_mix_rd")
        s_var, s_y0, s_ln = sem("s_var"), sem("s_y0"), sem("s_ln")
        s_h1, s_resid, s_y = sem("s_h1"), sem("s_resid"), sem("s_y")
        s_res, s_badj = sem("s_res"), sem("s_badj")
        s_qk, s_qk_hi, s_qk_lo = sem("s_qk"), sem("s_qk_hi"), sem("s_qk_lo")
        s_stack = [sem(f"s_stack{j}") for j in range(6)]
        s_v, s_v_hi, s_v_rd, s_v_all, s_v_mid = sem("s_v"), sem("s_v_hi"), sem("s_v_rd"), sem("s_v_all"), sem("s_v_mid")
        s_sc, s_msk, s_prob = sem("s_sc"), sem("s_msk"), sem("s_prob")
        s_pt, s_pt_hi, s_pt_lo = sem("s_pt"), sem("s_pt_hi"), sem("s_pt_lo")
        s_pv, s_att = sem("s_pv"), sem("s_att")
        s_out_ok, s_out = sem("s_out_ok"), sem("s_out")
        s_apart = sem("s_apart")
        s_dve, s_pool = sem("s_dve"), sem("s_pool")

        def wait(eng, s, count):
            if not (isinstance(count, int) and count <= 0):
                eng.wait_ge(s, count)

        def apart(eng):
            eng.sem_inc(s_apart, 1)

        STACKED = 16 * SLOTS * HPG

        def layer_a(t):
            return 2 * t

        def layer_b(t):
            return 2 * t - 1

        def norm_index(t, kind):
            if isinstance(t, int):
                if t == 0:
                    return 0
                if t == NB + 1:
                    return 4 * NB - 1
                if t == NB and kind == "c":
                    return 4 * NB - 4 + 2
            return 4 * t - 4 + {"b": 0, "b2": 1, "a": 2, "c": 3}[kind] + (1 if isinstance(t, int) and t == 1 else 0)

        def run(steps, todo, t):
            for name, k in todo:
                if name in steps:
                    steps[name](t, k)

        def pipeline(eng, body):
            body(0, schedule(True, False, False))
            body(1, schedule(True, True, False))
            body(2, schedule(True, True, True))
            with eng.Fori(3, NB) as t:
                body(t, schedule(True, True, True))
            body(NB, schedule(False, True, True))
            body(NB + 1, schedule(False, False, True))

        block = ctx.enter_context(nc.Block())

        @block.sync
        def _(sp):
            for l in range(LAYERS):
                for m, b in enumerate((bl, bs, br)):
                    for half in range(2):
                        r = 64 * l + 32 * half
                        sp.dma_start(self_part[r:r + 1, :, :].rearrange("p i d -> p (i d)")[:, 0:D] if m == 0 else
                                     (self_part[r:r + 1, 1, :] if m == 1 else mixed[r:r + 1, 0, :]),
                                     b[l:l + 1, :]).then_inc(s_const, 16)
            sp.dma_start(q_bias[:, :], bq.rearrange("(g p) -> p g", p=P), allow_slow_non_contiguous=True).then_inc(s_const, 16)
            sp.dma_start(k_bias[:, :], bk.rearrange("(g p) -> p g", p=P), allow_slow_non_contiguous=True).then_inc(s_const, 16)
            sp.dma_start(g1_col[:, :], ln_w[0, :].rearrange("(g p) -> p g", p=P), allow_slow_non_contiguous=True).then_inc(s_const, 16)
            sp.dma_start(b1_col[:, :], ln_b[0, :].rearrange("(g p) -> p g", p=P), allow_slow_non_contiguous=True).then_inc(s_const, 16)
            sp.dma_start(v_bias[:, :], bv.partition_broadcast(P)).then_inc(s_const, 16)
            sp.dma_start(g2_row[:, :], ln_w[1, :].partition_broadcast(P)).then_inc(s_const, 16)
            sp.dma_start(b2_row[:, :], ln_b[1, :].partition_broadcast(P)).then_inc(s_const, 16)
            sp.dma_start(beta_col[:, :], beta.partition_broadcast(P)).then_inc(s_const, 16)

            sp.wait_ge(s_setup, 1)

            def body(t, todo):
                names = [n for n, _ in todo]
                in_a, in_b, in_c = "a_scores" in names, "b_scores" in names, "final" in names
                if in_c:
                    wait(sp, s_em, 2 * (layer_a(t - 1) + 1) if not (isinstance(t, int) and t > NB)
                         else 2 * (layer_b(t - 1) + 1))
                    apart(sp)
                    sp.dma_start(adj_in[:, :, :], adj_v[t - 2]).then_inc(s_adj["c"], 16)
                if in_a:
                    wait(sp, s_resid, (t - 1) * NT)
                    if isinstance(t, int) and t == 1:
                        sp.wait_ge(s_tx_pe, NC)
                    apart(sp)
                    sp.dma_start(x_in[:, :, :], x_v[t]).then_inc(s_xa, 16)
                if in_c:
                    c = t - 2
                    for j in range(2 * NC):
                        wait(sp, s_qk_lo, 6 * c + j + 1)
                        apart(sp)
                        dst = (q_st, k_st)[j % 2]
                        parts = ((qk_hi, qk_lo, qk_hi), (qk_hi, qk_hi, qk_lo))[j % 2]
                        for slot in range(SLOTS):
                            for r in range(HPG):
                                head = HPG * (j // 2) + r
                                sp.dma_start(dst[slot * HD:(slot + 1) * HD, head, :].bitcast(F32),
                                             parts[slot][r * HD:(r + 1) * HD, j % RING, :].bitcast(F32)
                                             ).then_inc(s_stack[j], 16)
                if in_b:
                    if in_c:
                        wait(sp, s_badj, t - 1)
                    else:
                        wait(sp, s_em, 2 * (layer_a(t - 1) + 1))
                    apart(sp)
                    sp.dma_start(adj_in[:, :, :], adj_v[t - 1]).then_inc(s_adj["b"], 16)
                    if in_a:
                        wait(sp, s_tx_pe, NC * (t + 1))
                    else:
                        wait(sp, s_resid, (t - 1) * NT)
                    apart(sp)
                    sp.dma_start(x_in[:, :, :], x_v[t - 1]).then_inc(s_xb, 16)
                if in_a:
                    if in_b:
                        wait(sp, s_em, 2 * (layer_b(t) + 1))
                    apart(sp)
                    sp.dma_start(adj_in[:, :, :], adj_v[t]).then_inc(s_adj["a"], 16)
                if in_c:
                    sp.wait_ge(s_out_ok, (t - 1) * NT)
                    apart(sp)
                    sp.dma_start(out_v[t - 2], result[:, :, :]).then_inc(s_out, 16)

            pipeline(sp, body)
            sp.wait_ge(s_out, 16 * NB)

        @block.tensor
        def _(pe):
            def mm(dst, lhsT, rhs, start, stop):
                return nc.tensor.matmul(dst, lhsT, rhs, start=start, stop=stop)

            def turn_x(t, k):
                pe.wait_ge(s_xa, 16 * (t + 1))
                wait(pe, s_th_lo, NC * t) if k == 0 else None
                wait(pe, s_tx_lo, NC * t + k)
                for i in range(NT):
                    last = nc.tensor.transpose(bank_t[:, i * P:(i + 1) * P], x_in[:, i, k * P:(k + 1) * P], ident[:, :])
                last.then_inc(s_tx_pe, 1)

            def turn_h(t, k):
                pe.wait_ge(s_h1, NT * t)
                if k == 0:
                    wait(pe, s_ty_lo, NC * (t - 1))
                    pe.wait_ge(s_tx_lo, NC * t)
                wait(pe, s_th_lo, NC * (t - 1) + k)
                for i in range(NT):
                    last = nc.tensor.transpose(bank_t[:, i * P:(i + 1) * P], normed[:, i, k * P:(k + 1) * P], ident[:, :])
                last.then_inc(s_th_pe, 1)

            def turn_y(t, k):
                pe.wait_ge(s_y, NT * t)
                if k == 0:
                    pe.wait_ge(s_th_lo, NC * t)
                    if not (isinstance(t, int) and t == NB):
                        pe.wait_ge(s_tx_lo, NC * (t + 1))
                wait(pe, s_ty_lo, NC * (t - 1) + k)
                for i in range(NT):
                    last = nc.tensor.transpose(bank_t[:, i * P:(i + 1) * P], y_in[:, i, k * P:(k + 1) * P], ident[:, :])
                last.then_inc(s_ty_pe, 1)

            def graph_scores(n, hT, ready):
                ready()
                wait(pe, s_at_lo, n)
                for i in range(NT):
                    for c in range(NC):
                        for a, b in PARTS:
                            last = mm(bank_u[:, i * S:(i + 1) * S], hT[a][:, c, i * P:(i + 1) * P], hT[b][:, c, :],
                                      c == 0 and (a, b) == PARTS[0], c == NC - 1 and (a, b) == PARTS[-1])
                last.then_inc(s_u, 1)

            def a_scores(t, _k):
                graph_scores(layer_a(t), hT_ac, lambda: pe.wait_ge(s_tx_lo, NC * (t + 1)))

            def b_scores(t, _k):
                graph_scores(layer_b(t), hT_b, lambda: pe.wait_ge(s_th_lo, NC * t))

            def projection(n, layer, hT, j):
                m, i = j // 2, j % 2
                if j >= 2:
                    pe.wait_ge(s_proj_rd, 6 * n + j - 1)
                for c in range(NC):
                    for a, b in PARTS:
                        mm(bank_w[i][:, 0:D], hT[a][:, c, i * P:(i + 1) * P], w_graph[layer][b][:, c, m, :],
                           c == 0 and (a, b) == PARTS[0], False)
                mm(bank_w[i][:, 0:D], pick_bias[layer][:, :], bias_rows[:, m, :], False, True).then_inc(s_proj, 1)

            def a_proj(t, j):
                if j < 2:
                    wait(pe, s_proj_rd, 6 * layer_a(t) - 1 + j)
                projection(layer_a(t), 0, hT_ac, j)

            def b_proj(t, j):
                if j < 2:
                    wait(pe, s_proj_rd, 6 * layer_b(t) - 1 + j)
                    wait(pe, s_v_rd, NT * (t - 1) - 1 + j)
                projection(layer_b(t), 1, hT_b, j)

            def graph_turn(n):
                pe.wait_ge(s_em, 2 * (n + 1))
                for j in range(NT):
                    for i in range(NT):
                        last = nc.tensor.transpose(bank_u[:, j * S + i * P:j * S + (i + 1) * P],
                                                   expu[:, i, j * P:(j + 1) * P], ident[:, :])
                last.then_inc(s_at, 1)

            def mix(n, i):
                pe.wait_ge(s_cut, n + 1)
                pe.wait_ge(s_proj_rd, 6 * (n + 1))
                wait(pe, s_mix_rd, 2 * n + i)
                other = 1 - i
                terms = ([(up, i, None, i, 0)], [(low, i, None, i, 1)],
                         [(attT, other, i, other, 0 if i == 0 else 1)])
                terms = [x[0] for x in terms]
                count = 0
                for src, jb, ib, j, side in terms:
                    for a, b in PARTS:
                        w = src[a][:, jb, :] if ib is None else src[a][:, jb, ib * P:(ib + 1) * P]
                        last = mm(bank_m[:, 0:D], w, hlr[b][:, j, side, :], count == 0, count == 8)
                        count += 1
                last.then_inc(s_mix, 1)

            def qk(t, j):
                s = t - 2
                g = j // 2
                if j == 0:
                    pe.wait_ge(s_ty_lo, NC * (t - 1))
                if j < 2:
                    if isinstance(t, int) and t == NB + 1:
                        pe.wait_ge(s_proj_rd, 6 * layer_b(t - 1) + 5 + j)
                    else:
                        pe.wait_ge(s_proj_rd, 6 * layer_a(t - 1) + 5 + j)
                else:
                    pe.wait_ge(s_qk_lo, 6 * s + j - 1)
                for c in range(NC):
                    for a, b in PARTS:
                        last = mm(bank_w[j % 2][:, 0:S], w_qkv[a][:, c, j % 2, g * P:(g + 1) * P], hT_ac[b][:, c, :],
                                  c == 0 and (a, b) == PARTS[0], c == NC - 1 and (a, b) == PARTS[-1])
                last.then_inc(s_qk, 1)

            def v(t, i):
                s = t - 2
                pe.wait_ge(s_qk_lo, 6 * s + 5 + i)
                for c in range(NC):
                    for a, b in PARTS:
                        last = mm(bank_w[i][:, 0:D], hT_ac[a][:, c, i * P:(i + 1) * P], w_qkv[b][:, c, 2, :],
                                  c == 0 and (a, b) == PARTS[0], c == NC - 1 and (a, b) == PARTS[-1])
                last.then_inc(s_v, 1)

            def scores(t, h):
                s = t - 2
                if h % HPG == 0:
                    for j in (2 * (h // HPG), 2 * (h // HPG) + 1):
                        pe.wait_ge(s_stack[j], STACKED * (s + 1))
                wait(pe, s_msk, NT * (NH * s + h))
                for i in range(NT):
                    last = mm(bank_s[:, i * S:(i + 1) * S], q_st[0:SLOTS * HD, h, i * P:(i + 1) * P],
                              k_st[0:SLOTS * HD, h, :], True, True)
                last.then_inc(s_sc, 1)

            def weights(t, h):
                s = t - 2
                pe.wait_ge(s_prob, NT * (NH * s + h + 1))
                wait(pe, s_pt_lo, NH * s + h)
                for j in range(NT):
                    for i in range(NT):
                        last = nc.tensor.transpose(bank_p[:, j * S + i * P:j * S + (i + 1) * P],
                                                   prob[:, h % 2, i, j * P:(j + 1) * P], ident[:, :])
                last.then_inc(s_pt, 1)

            def attend(t, h):
                s = t - 2
                pe.wait_ge(s_pt_lo, NH * s + h + 1)
                if h == 0:
                    pe.wait_ge(s_v_all, NT * (s + 1))
                if h % 2 == 0:
                    wait(pe, s_att, (NH * s + h) // 2 if isinstance(s, int) else NH // 2 * s + h // 2)
                for i in range(NT):
                    at = (NT * (h % 2) + i) * VP * HD
                    for j in range(NT):
                        vp = v_parts[:, j, h, :, :].rearrange("p a d -> p (a d)")
                        mm(bank_o[:, at:at + VP * HD], pT_hi[:, h % 2, j, i * P:(i + 1) * P], vp, j == 0, False)
                        last = mm(bank_o[:, at:at + 2 * HD], pT_lo[:, h % 2, j, i * P:(i + 1) * P], vp[:, 0:2 * HD],
                                  False, j == NT - 1)
                last.then_inc(s_pv, 1)

            steps = {
                "turn_x": turn_x, "turn_h": turn_h, "turn_y": turn_y,
                "a_scores": a_scores, "b_scores": b_scores, "a_proj": a_proj, "b_proj": b_proj,
                "a_turn": lambda t, k: graph_turn(layer_a(t)), "b_turn": lambda t, k: graph_turn(layer_b(t)),
                "a_mix": lambda t, k: mix(layer_a(t), k), "b_mix": lambda t, k: mix(layer_b(t), k),
                "qk": qk, "v": v, "scores": scores, "weights": weights, "attend": attend,
            }
            pe.wait_ge(s_setup, 1)
            pipeline(pe, lambda t, todo: run(steps, todo, t))

        @block.scalar
        def _(act):
            nc.scalar.preload_act_table_set("natural_log_exp_and_others")

            for n, (mats, l) in enumerate((((wl, ws, wr), 0), ((wl, ws, wr), 1), ((wq, wk, wv), None))):
                wait(act, s_split, 18 * n)
                for m, w in enumerate(mats):
                    for c in range(NC):
                        src = (w[l] if l is not None else w)[c * P:(c + 1) * P, :]
                        act.dma_start(staging[NC * m + c], src).then_inc(s_stage, 16)

            def turn_x(t, k):
                act.wait_ge(s_tx_pe, NC * t + k + 1)
                if k == 0:
                    wait(act, s_v, NT * (t - 1))
                nc.scalar.activation(hT_ac[0][:, k, :], bank_t[:, 0:S], ACT.Copy).then_inc(s_tx_hi, 1)

            def turn_y(t, k):
                act.wait_ge(s_ty_pe, NC * (t - 1) + k + 1)
                if k == 0 and not (isinstance(t, int) and t == NB):
                    act.wait_ge(s_proj, 6 * layer_a(t) + 6)
                nc.scalar.activation(hT_ac[0][:, k, :], bank_t[:, 0:S], ACT.Copy).then_inc(s_ty_hi, 1)

            def turn_h(t, k):
                act.wait_ge(s_th_pe, NC * (t - 1) + k + 1)
                nc.scalar.activation(mixed[:, 0, 0:S] if k == 0 else (mixed[:, 1, 0:S] if k == 1 else self_part[:, 0, 0:S]),
                                     bank_t[:, 0:S], ACT.Relu, bias=b1_col[:, k:k + 1],
                                     scale=g1_col[:, k:k + 1]).then_inc(s_th_f, 1)

            def graph_exp(n):
                act.wait_ge(s_ub, n + 1)
                wait(act, s_at, n)
                for i in range(NT):
                    nc.scalar.activation(expu[:, i, :], bank_u[:, i * S:(i + 1) * S], ACT.Exp, bias=ubias[:, i:i + 1],
                                         scale=TEMPER, accum_out=zsum[:, i:i + 1]).then_inc(s_exp, 1)

            def proj_hi(n, j):
                m, i = j // 2, j % 2
                if m != 1:
                    act.wait_ge(s_proj, 6 * n + j + 1)
                    if j == 0:
                        wait(act, s_mix, 2 * n)
                    nc.scalar.activation(hlr[0][:, i, m // 2, :], bank_w[i][:, 0:D], ACT.Copy).then_inc(s_proj_hi, 1)

            def graph_turn(n):
                act.wait_ge(s_at, n + 1)
                wait(act, s_mix, 2 * n)
                wait(act, s_cut, n)
                nc.scalar.activation(attT[0][:, :, :].rearrange("p j i -> p (j i)"), bank_u[:, :], ACT.Copy).then_inc(s_at_hi, 1)

            def root(index):
                act.wait_ge(s_var, index + 1)
                nc.scalar.activation(lnv[:, :], var[:, :], ACT.Ln).then_inc(s_ln, 1)
                act.wait_ge(s_ln, index + 1)
                nc.scalar.activation(y0[:, :], lnv[:, :], ACT.Exp, scale=-0.5).then_inc(s_y0, 1)

            def qk(t, j):
                s = t - 2
                act.wait_ge(s_qk, 6 * s + j + 1)
                wait(act, s_stack[(j + RING) % 6], STACKED * (s if j < RING else s + 1))
                nc.scalar.activation(qk_hi[:, j % RING, :], bank_w[j % 2][:, 0:S], ACT.Identity,
                                     bias=(q_bias, k_bias)[j % 2][:, j // 2:j // 2 + 1]).then_inc(s_qk_hi, 1)

            def v(t, i):
                s = t - 2
                act.wait_ge(s_v, NT * s + i + 1)
                if i == 0:
                    wait(act, s_pv, NH * s)
                nc.scalar.activation(v_parts[:, i, :, 0, :], bank_w[i][:, 0:D].rearrange("p (h d) -> p h d", h=NH),
                                     ACT.Copy).then_inc(s_v_hi, 1)

            def scores(t, h):
                s = t - 2
                wait(act, s_pt, NH * s + max(h - 1, 0))
                for i in range(NT):
                    act.wait_ge(s_msk, NT * (NH * s + h) + i + 1)
                    nc.scalar.activation(prob[:, h % 2, i, :], masked[:, i, :], ACT.Exp, bias=hmin[:, i, h:h + 1],
                                         scale=-1.0, accum_out=hsum[:, i, h:h + 1]).then_inc(s_prob, 1)

            def weights(t, h):
                s = t - 2
                act.wait_ge(s_pt, NH * s + h + 1)
                wait(act, s_pv, NH * s + max(h - 1, 0))
                nc.scalar.activation(pT_hi[:, h % 2, :, :].rearrange("p j i -> p (j i)"), bank_p[:, :], ACT.Copy).then_inc(s_pt_hi, 1)

            steps = {
                "turn_x": turn_x, "turn_h": turn_h, "turn_y": turn_y,
                "a_scores": lambda t, k: graph_exp(layer_a(t)), "b_scores": lambda t, k: graph_exp(layer_b(t)),
                "a_proj": lambda t, k: proj_hi(layer_a(t), k), "b_proj": lambda t, k: proj_hi(layer_b(t), k),
                "a_turn": lambda t, k: graph_turn(layer_a(t)), "b_turn": lambda t, k: graph_turn(layer_b(t)),
                "a_norm": lambda t, k: root(norm_index(t, "a")), "b_norm": lambda t, k: root(norm_index(t, "b")),
                "b_norm2": lambda t, k: root(norm_index(t, "b2")), "final": lambda t, k: root(norm_index(t, "c")),
                "qk": qk, "v": v, "scores": scores, "weights": weights,
            }
            pipeline(act, lambda t, todo: run(steps, todo, t))

        @block.vector
        def _(dve):
            ve = nc.vector
            links = [0, 0]

            def link(ins):
                ins.then_inc(s_dve, 1)
                links[1] += 1
                dve.wait_ge(s_dve, links[0] + links[1])

            for n, w in enumerate((w_graph[0], w_graph[1], w_qkv)):
                dve.wait_ge(s_stage, 16 * 9 * (n + 1))
                for k in range(9):
                    m, c = k // NC, k % NC
                    ve.tensor_copy(w[0][:, c, m, :], staging[k]).then_inc(s_split, 1)
                    dve.wait_ge(s_split, 18 * n + 2 * k + 1)
                    ve.tensor_tensor(w[1][:, c, m, :], staging[k], w[0][:, c, m, :], ALU.subtract).then_inc(s_split, 1)
            dve.wait_ge(s_pool_c, 8)
            dve.wait_ge(s_const, 16 * 20)
            srcs = (self_part[:, 0, :], self_part[:, 1, :], mixed[:, 0, :])
            for l in range(LAYERS):
                for half in range(2):
                    r = 64 * l + 32 * half
                    link(ve.memset(pick_bias[l][r:r + 1, :].bitcast(F32), 1.0))
            for m in range(3):
                for l in range(LAYERS):
                    r = 64 * l
                    link(ve.tensor_copy(bias_rows[r:r + 1, m, :], srcs[m][r:r + 1, :]))
                    link(ve.tensor_copy(bias_rows[r + 32:r + 33, m, :], srcs[m][r + 32:r + 33, :]))
                    link(ve.tensor_tensor(bias_rows[r + 32:r + 33, m, :], srcs[m][r + 32:r + 33, :],
                                          bias_rows[r + 32:r + 33, m, :], ALU.subtract))
            dve.wait_ge(s_split, 54)
            ve.tensor_scalar(beta_col[:, :], beta_col[:, :], 1.0 / SCALE, None, ALU.mult).then_inc(s_setup, 1)
            dve.wait_ge(s_setup, 1)

            def turn_x(t, k):
                dve.wait_ge(s_tx_hi, NC * t + k + 1)
                ve.tensor_tensor(hT_ac[1][:, k, :], bank_t[:, 0:S], hT_ac[0][:, k, :], ALU.subtract).then_inc(s_tx_lo, 1)

            def turn_y(t, k):
                dve.wait_ge(s_ty_hi, NC * (t - 1) + k + 1)
                ve.tensor_tensor(hT_ac[1][:, k, :], bank_t[:, 0:S], hT_ac[0][:, k, :], ALU.subtract).then_inc(s_ty_lo, 1)

            def turn_h(t, k):
                dve.wait_ge(s_th_f, NC * (t - 1) + k + 1)
                f = mixed[:, 0, 0:S] if k == 0 else (mixed[:, 1, 0:S] if k == 1 else self_part[:, 0, 0:S])
                link(ve.tensor_copy(hT_b[0][:, k, :], f))
                ve.tensor_tensor(hT_b[1][:, k, :], f, hT_b[0][:, k, :], ALU.subtract).then_inc(s_th_lo, 1)

            def graph_scores(n, s_loaded, count):
                dve.wait_ge(s_u, n + 1)
                link(ve.tensor_reduce(negmax[:, :], bank_u[:, :].rearrange("p (i j) -> p i j", i=NT), AX.X, ALU.max, negate=True))
                ve.tensor_scalar(ubias[:, :], negmax[:, :], TEMPER, None, ALU.mult).then_inc(s_ub, 1)

            def graph_mask(n, s_loaded, count):
                dve.wait_ge(s_loaded, count)
                for i in range(NT):
                    dve.wait_ge(s_exp, 2 * n + i + 1)
                    ve.scalar_tensor_tensor(expu[:, i, :], expu[:, i, :], 1.0, adj_in[:, i, :], ALU.mult, ALU.mult,
                                            accum_out=ssum[:, i:i + 1]).then_inc(s_em, 1)
                dve.wait_ge(s_em, 2 * (n + 1))
                for i in range(NT):
                    link(ve.scalar_tensor_tensor(diag_tmp[:, :], expu[:, i, i * P:(i + 1) * P], 1.0, ident[:, :],
                                                 ALU.mult, ALU.mult, accum_out=diag[:, i:i + 1]))
                link(ve.scalar_tensor_tensor(inv_s[:, :], zsum[:, :], EPS_ATTN, ssum[:, :], ALU.mult, ALU.add))
                link(ve.reciprocal(inv_s[:, :], inv_s[:, :]))

            def projection(n, j):
                m, i = j // 2, j % 2
                if m == 1:
                    dve.wait_ge(s_proj, 6 * n + j + 1)
                    ve.tensor_scalar(self_part[:, i, :], bank_w[i][:, 0:D], diag[:, i:i + 1], None,
                                     ALU.mult).then_inc(s_proj_rd, 1)
                else:
                    dve.wait_ge(s_proj_hi, 4 * n + (j if m == 0 else j - 2) + 1)
                    ve.tensor_tensor(hlr[1][:, i, m // 2, :], bank_w[i][:, 0:D], hlr[0][:, i, m // 2, :],
                                     ALU.subtract).then_inc(s_proj_rd, 1)

            def graph_turn(n):
                dve.wait_ge(s_at_hi, n + 1)
                ve.tensor_tensor(attT[1][:, :, :].rearrange("p j i -> p (j i)"), bank_u[:, :],
                                 attT[0][:, :, :].rearrange("p j i -> p (j i)"), ALU.subtract).then_inc(s_at_lo, 1)

            def mix(n, i):
                dve.wait_ge(s_mix, 2 * n + i + 1)
                dve.wait_ge(s_proj_rd, 6 * n + 4)
                ve.tensor_tensor(mixed[:, i, :], bank_m[:, 0:D], self_part[:, i, :], ALU.add).then_inc(s_mix_rd, 1)
                dve.wait_ge(s_mix_rd, 2 * n + i + 1)
                link(ve.bn_stats(stats[:, i, :], mixed[:, i, :]))
                apart(dve)
                link(ve.bn_aggr(mv[:, i, :], stats[:, i, :]))

            def refine(index):
                dve.wait_ge(s_y0, index + 1)
                link(ve.tensor_tensor(tmp[:, :], y0[:, :], y0[:, :], ALU.mult))
                link(ve.tensor_tensor(tmp[:, :], tmp[:, :], var[:, :], ALU.mult))
                link(ve.tensor_scalar(tmp[:, :], tmp[:, :], -0.5, 1.5, ALU.mult, ALU.add))
                link(ve.tensor_tensor(rstd[:, :], tmp[:, :], y0[:, :], ALU.mult))

            def graph_norm(index):
                link(ve.tensor_tensor(tmp[:, :], mv[:, :, 1], inv_s[:, :], ALU.mult))
                link(ve.tensor_tensor(tmp[:, :], tmp[:, :], inv_s[:, :], ALU.mult))
                ve.tensor_scalar(var[:, :], tmp[:, :], EPS_GRAPH, None, ALU.add).then_inc(s_var, 1)
                refine(index)
                link(ve.tensor_tensor(rstd[:, :], rstd[:, :], inv_s[:, :], ALU.mult))

            def a_norm(t, _k):
                graph_norm(norm_index(t, "a"))
                for i in range(NT):
                    ve.tensor_scalar(normed[:, i, :], mixed[:, i, :], mv[:, i, 0:1], rstd[:, i:i + 1],
                                     ALU.subtract, ALU.mult).then_inc(s_h1, 1)

            def b_norm(t, _k):
                graph_norm(norm_index(t, "b"))
                for i in range(NT):
                    link(ve.scalar_tensor_tensor(normed[:, i, :], mixed[:, i, :], mv[:, i, 0:1], g2_row[:, :],
                                                 ALU.subtract, ALU.mult))
                    link(ve.scalar_tensor_tensor(normed[:, i, :], normed[:, i, :], rstd[:, i:i + 1], b2_row[:, :],
                                                 ALU.mult, ALU.add))
                    if i == 0:
                        dve.wait_ge(s_xb, 16 * t)
                    ve.scalar_tensor_tensor(mixed[:, i, :], normed[:, i, :], 0.0, x_in[:, i, :],
                                            ALU.max, ALU.add).then_inc(s_resid, 1)
                    dve.wait_ge(s_resid, NT * (t - 1) + i + 1)
                    link(ve.bn_stats(stats[:, i, :], mixed[:, i, :]))
                    apart(dve)
                    link(ve.bn_aggr(mv[:, i, :], stats[:, i, :]))
                ve.tensor_scalar(var[:, :], mv[:, :, 1], EPS_NORM, None, ALU.add).then_inc(s_var, 1)

            def b_norm2(t, _k):
                refine(norm_index(t, "b2"))
                wait(dve, s_res, t - 1 if not (isinstance(t, int) and t == 1) else 0)
                for i in range(NT):
                    ve.tensor_scalar(y_in[:, i, :], mixed[:, i, :], mv[:, i, 0:1], rstd[:, i:i + 1],
                                     ALU.subtract, ALU.mult).then_inc(s_y, 1)

            def qk(t, j):
                s = t - 2
                dve.wait_ge(s_qk_hi, 6 * s + j + 1)
                ve.scalar_tensor_tensor(qk_lo[:, j % RING, :], bank_w[j % 2][:, 0:S],
                                        (q_bias, k_bias)[j % 2][:, j // 2:j // 2 + 1],
                                        qk_hi[:, j % RING, :], ALU.add, ALU.subtract).then_inc(s_qk_lo, 1)

            def v(t, i):
                s = t - 2
                dve.wait_ge(s_v_hi, NT * s + i + 1)
                ve.tensor_tensor(v_rest[:, i, :].rearrange("p (h d) -> p h d", h=NH),
                                 bank_w[i][:, 0:D].rearrange("p (h d) -> p h d", h=NH),
                                 v_parts[:, i, :, 0, :], ALU.subtract).then_inc(s_v_rd, 1)

            def scores(t, h):
                s = t - 2
                dve.wait_ge(s_sc, NH * s + h + 1)
                if h == 0:
                    dve.wait_ge(s_badj, s + 1)
                wait(dve, s_prob, NT * (NH * s + h))
                apart(dve)
                for i in range(NT):
                    ve.tensor_tensor_reduce(masked[:, i, :], bank_s[:, i * S:(i + 1) * S], bias_adj[:, i, :],
                                            -SCALE, BIG, ALU.add, ALU.min, hmin[:, i, h:h + 1]).then_inc(s_msk, 1)

            def weights(t, h):
                s = t - 2
                dve.wait_ge(s_pt_hi, NH * s + h + 1)
                ve.tensor_tensor(pT_lo[:, h % 2, :, :].rearrange("p j i -> p (j i)"), bank_p[:, :],
                                 pT_hi[:, h % 2, :, :].rearrange("p j i -> p (j i)"), ALU.subtract).then_inc(s_pt_lo, 1)

            def attend(t, h):
                if h % 2 == 1:
                    s = t - 2
                    dve.wait_ge(s_pv, NH * s + h + 1)
                    for k in range(2):
                        at = k * NT * VP * HD
                        ins = ve.tensor_reduce(att[:, :, h - 1 + k, :],
                                               bank_o[:, at:at + NT * VP * HD].rearrange("p (i a d) -> p i d a", i=NT, a=VP),
                                               AX.X, ALU.add)
                        if k == 0:
                            link(ins)
                    ins.then_inc(s_att, 1)

            def final(t, _k):
                s = t - 2
                dve.wait_ge(s_prob, NT * NH * (s + 1))
                link(ve.reciprocal(hinv[:, :, :], hsum[:, :, :]))
                dve.wait_ge(s_att, NH // 2 * (s + 1))
                dve.wait_ge(s_res, s + 1)
                wait(dve, s_out, 16 * s)
                for i in range(NT):
                    link(ve.tensor_tensor(att[:, i, :, :], att[:, i, :, :],
                                          hinv[:, i, :].unsqueeze(2).to_broadcast([P, NH, HD]), ALU.mult))
                    link(ve.tensor_tensor(result[:, i, :], att[:, i, :, :].rearrange("p h d -> p (h d)"), res[:, i, :], ALU.add))
                    link(ve.bn_stats(stats[:, i, :], result[:, i, :]))
                    apart(dve)
                    link(ve.bn_aggr(mv[:, i, :], stats[:, i, :]))
                ve.tensor_scalar(var[:, :], mv[:, :, 1], EPS_NORM, None, ALU.add).then_inc(s_var, 1)
                refine(norm_index(t, "c"))
                for i in range(NT):
                    ve.tensor_scalar(result[:, i, :], result[:, i, :], mv[:, i, 0:1], rstd[:, i:i + 1],
                                     ALU.subtract, ALU.mult).then_inc(s_out_ok, 1)

            def a_scores(t, _k):
                graph_scores(layer_a(t), s_adj["a"], 16 * (t + 1))
                graph_mask(layer_a(t), s_adj["a"], 16 * (t + 1))

            def b_scores(t, _k):
                graph_scores(layer_b(t), s_adj["b"], 16 * t)
                graph_mask(layer_b(t), s_adj["b"], 16 * t)

            steps = {
                "turn_x": turn_x, "turn_h": turn_h, "turn_y": turn_y,
                "a_scores": a_scores, "b_scores": b_scores,
                "a_proj": lambda t, k: projection(layer_a(t), k), "b_proj": lambda t, k: projection(layer_b(t), k),
                "a_turn": lambda t, k: graph_turn(layer_a(t)), "b_turn": lambda t, k: graph_turn(layer_b(t)),
                "a_mix": lambda t, k: mix(layer_a(t), k), "b_mix": lambda t, k: mix(layer_b(t), k),
                "a_norm": a_norm, "b_norm": b_norm, "b_norm2": b_norm2, "final": final,
                "qk": qk, "v": v, "scores": scores, "weights": weights, "attend": attend,
            }
            PER_ITERATION = 66

            def body(t, todo):
                if not isinstance(t, int):
                    links[0] = links[0] + links[1] + (t - 3) * PER_ITERATION
                    links[1] = 0
                run(steps, todo, t)
                if not isinstance(t, int):
                    assert links[1] == PER_ITERATION, links[1]
                    links[0], links[1] = base[0] + (NB - 3) * PER_ITERATION, 0
                else:
                    links[0], links[1] = links[0] + links[1], 0
                    base[0] = links[0]

            base = [0]
            pipeline(dve, body)

        @block.gpsimd
        def _(pool):
            gp = nc.gpsimd
            gp.memset(bias_rows[:, :, :].bitcast(F32), 0.0).then_inc(s_pool_c, 1)
            for l in range(LAYERS):
                gp.memset(pick_bias[l][:, :].bitcast(F32), 0.0).then_inc(s_pool_c, 1)
            gp.memset(ident[:, :], 1.0).then_inc(s_pool_c, 1)
            gp.memset(mask_up[:, :], 1.0).then_inc(s_pool_c, 1)
            pool.wait_ge(s_pool_c, 5)
            gp.affine_select(out=ident[:, :], in_=ident[:, :], pattern=[[-1, P]], compare_op=ALU.is_equal, fill=0.0,
                             base=0, channel_multiplier=1).then_inc(s_pool_c, 1)
            gp.affine_select(out=mask_low[:, :], in_=mask_up[:, :], pattern=[[1, P]], compare_op=ALU.is_gt, fill=0.0,
                             base=0, channel_multiplier=-1).then_inc(s_pool_c, 1)
            pool.wait_ge(s_pool_c, 7)
            gp.affine_select(out=mask_up[:, :], in_=mask_up[:, :], pattern=[[-1, P]], compare_op=ALU.is_gt, fill=0.0,
                             base=0, channel_multiplier=1).then_inc(s_pool_c, 1)
            pool.wait_ge(s_pool_c, 8)
            pool.wait_ge(s_setup, 1)

            def graph_turn(n):
                pool.wait_ge(s_at_lo, n + 1)
                wait(pool, s_mix, 2 * n)
                for part in range(2):
                    blocks = attT[part][:, :, :].rearrange("p j (i q) -> p (j i) q", i=NT)[:, 0::3, :]
                    for dst, keep in ((up, mask_up), (low, mask_low)):
                        ins = gp.tensor_tensor(dst[part][:, :, :], blocks,
                                               keep[:, :].unsqueeze(1).to_broadcast([P, NT, P]), ALU.mult)
                ins.then_inc(s_cut, 1)

            def qk(t, j):
                s = t - 2
                if j == 0:
                    pool.wait_ge(s_adj["c"], 16 * (s + 1))
                    wait(pool, s_msk, NT * NH * s)
                    apart(pool)
                    gp.tensor_scalar(neg_adj[:, :, :], adj_in[:, :, :], 0.0, MASKED / SCALE, ALU.is_le, ALU.mult
                                     ).then_inc(s_pool, 1)
                    gp.tensor_scalar(bias_adj[:, :, :], adj_in[:, :, :], 0.0, beta_col[:, 0:1], ALU.max, ALU.mult
                                     ).then_inc(s_pool, 1)
                    pool.wait_ge(s_pool, 2 * (s + 1))
                    gp.tensor_tensor(bias_adj[:, :, :], bias_adj[:, :, :], neg_adj[:, :, :], ALU.add).then_inc(s_badj, 1)
                if j == 2:
                    pool.wait_ge(s_y, NT * (s + 1))
                    wait(pool, s_out_ok, NT * s)
                    gp.tensor_tensor(res[:, :, :], y_in[:, :, :], v_bias[:, :].unsqueeze(1).to_broadcast([P, NT, D]),
                                     ALU.add).then_inc(s_res, 1)

            def v(t, i):
                s = t - 2
                pool.wait_ge(s_v_rd, NT * s + i + 1)
                wait(pool, s_pv, NH * s)
                apart(pool)
                rest = v_rest[:, i, :].rearrange("p (h d) -> p h d", h=NH)
                gp.tensor_copy(v_parts[:, i, :, 1, :], rest).then_inc(s_v_mid, 1)
                pool.wait_ge(s_v_mid, NT * s + i + 1)
                gp.tensor_tensor(v_parts[:, i, :, 2, :], rest, v_parts[:, i, :, 1, :], ALU.subtract).then_inc(s_v_all, 1)

            steps = {
                "a_turn": lambda t, k: graph_turn(layer_a(t)), "b_turn": lambda t, k: graph_turn(layer_b(t)),
                "qk": qk, "v": v,
            }
            pipeline(pool, lambda t, todo: run(steps, todo, t))


_WEIGHTS_T = ("L0_gnn_Wl", "L0_gnn_Ws", "L0_gnn_Wr")
_INS = ["x", "adj", "L0_gnn_Wl", "L0_gnn_Ws", "L0_gnn_Wr", "L0_gnn_bl", "L0_gnn_bs", "L0_gnn_br",
        "L0_gnn_ln_w", "L0_gnn_ln_b", "L1_gnn_Wq", "L1_gnn_Wk", "L1_gnn_Wv", "L1_gnn_bq", "L1_gnn_bk",
        "L1_gnn_bv", "L1_gnn_beta"]


def kernel(**inputs):
    import concourse.bacc as _bacc
    from concourse.bass_utils import run_bass_kernel_spmd as _run

    nc = _bacc.Bacc("TRN2", target_bir_lowering=False, num_devices=1)
    arrays, args = {}, []
    for name in _INS:
        a = np.asarray(inputs[name])
        if name in _WEIGHTS_T:
            a = a.transpose(0, 2, 1)
        if a.ndim == 0:
            a = a.reshape(1)
        a = np.ascontiguousarray(a)
        arrays[f"in_{name}"] = a
        args.append(nc.dram_tensor(f"in_{name}", a.shape, mybir.dt.from_np(a.dtype), kind="ExternalInput").ap())
    shape = arrays["in_x"].shape
    args.append(nc.dram_tensor("out_0", shape, F32, kind="ExternalOutput").ap())
    graph_attention_kernel(nc, *args)
    r = _run(nc, [arrays], core_ids=[0])
    return r.results[0]["out_0"]
```

```python
from contextlib import ExitStack

import numpy as np

import concourse.bass as bass
from concourse import mybir

F32 = mybir.dt.float32
F32R = mybir.dt.float32r
BF16 = mybir.dt.bfloat16
F16 = mybir.dt.float16
ALU = mybir.AluOpType
ACT = mybir.ActivationFunctionType
AX = mybir.AxisListType

P = 128
NH = 12
VP = 3
SLOTS = 3
EPS_GRAPH = 1e-12
EPS_NORM = 1e-5
EPS_ATTN = 1e-10
MASKED = -9000000000000000.0
BIG = 3.0e38
PARTS = ((0, 0), (0, 1), (1, 0))


def schedule(a, b, c, d):
    order = [
        (c, "q", 0), (d, "c_sum", 0), (c, "q", 1), (d, "c_norm", 0), (c, "q", 2), (c, "k", 0), (b, "turn_h", 0),
        (d, "c_apply", 0), (c, "k", 1), (b, "turn_h", 1), (c, "k", 2), (b, "turn_h", 2), (c, "v", 0), (c, "v", 1),
        (b, "b_scores", 0), (b, "b_proj", 0), (b, "b_proj", 1), (b, "b_mask", 0), (b, "b_proj", 2), (c, "head", 0),
        (b, "b_proj", 3), (c, "head", 1), (b, "b_turn", 0), (a, "turn_x", 0), (b, "b_proj", 4), (c, "head", 2),
        (a, "turn_x", 1), (b, "b_proj", 5), (c, "head", 3), (a, "turn_x", 2), (c, "head", 4), (b, "b_mix", 0),
        (a, "a_scores", 0), (c, "head", 5), (b, "b_mix", 1), (b, "b_norm", 0), (a, "a_proj", 0), (c, "head", 6),
        (b, "b_apply", 0), (a, "a_mask", 0), (a, "a_proj", 1), (c, "head", 7), (b, "b_out", 0), (a, "a_proj", 2),
        (c, "head", 8), (a, "a_turn", 0), (a, "a_proj", 3), (c, "head", 9), (a, "a_proj", 4), (c, "head", 10),
        (a, "a_proj", 5), (c, "head", 11), (b, "turn_y", 0), (a, "a_mix", 0), (b, "turn_y", 1), (c, "head", 12),
        (a, "a_mix", 1), (a, "a_norm", 0), (b, "turn_y", 2), (c, "head", 13), (a, "a_apply", 0),
    ]
    steps = []
    for on, name, k in order:
        if on and name == "head":
            steps += [(n, k - lag) for lag, n in enumerate(("scores", "weights", "attend")) if 0 <= k - lag < NH]
        elif on:
            steps.append((name, k))
    return steps


def graph_attention_kernel(nc, x, adj, wl, ws, wr, bl, bs, br, ln_w, ln_b,
                           wq, wk, wv, bq, bk, bv, beta, out):
    NB, S, D = x.shape
    NT = S // P
    NC = D // P
    HD = D // NH
    HPG = P // HD
    LAYERS = wl.shape[0]
    TEMPER = float(D) ** -0.5
    SCALE = float(HD) ** -0.5
    assert NT == 2 and NC == 3 and LAYERS == 2 and HD == 32

    x_v = x.rearrange("b (i p) d -> b p i d", p=P)
    adj_v = adj.rearrange("b (i p) j -> b p i j", p=P)
    out_v = out.rearrange("b (i p) d -> b p i d", p=P)

    with ExitStack() as ctx:
        def sb(name, shape, dt=F32):
            return ctx.enter_context(nc.sbuf_tensor(name, shape, dt))

        def bank(name):
            return ctx.enter_context(nc.psum_tensor(name, [P, 512], F32))

        def sem(name):
            return ctx.enter_context(nc.semaphore(name))

        w_graph = [[sb(f"w_graph{l}{p}", [P, NC, 3, D], F32R) for p in "hl"] for l in range(LAYERS)]
        w_qkv = [sb(f"w_qkv{p}", [P, NC, 3, D], F32R) for p in "hl"]
        bias_rows = sb("bias_rows", [P, 3, D], F32R)
        pick_bias = [sb(f"pick_bias{l}", [P, P], F32R) for l in range(LAYERS)]
        ident = sb("ident", [P, P])
        mask_up = sb("mask_up", [P, P])
        mask_low = sb("mask_low", [P, P])
        q_bias = sb("q_bias", [P, NC])
        k_bias = sb("k_bias", [P, NC])
        v_bias = sb("v_bias", [P, D])
        g1_col = sb("g1_col", [P, NC])
        b1_col = sb("b1_col", [P, NC])
        g2_row = sb("g2_row", [P, D])
        b2_row = sb("b2_row", [P, D])
        beta_col = sb("beta_col", [P, 1])
        x_in = sb("x_in", [P, NT, D])
        adj_in = sb("adj_in", [P, NT, S])
        hT_ac = [sb(f"hT_ac{p}", [P, NC, S], F32R) for p in "hl"]
        hT_b = [sb(f"hT_b{p}", [P, NC, S], F32R) for p in "hl"]
        expu = sb("expu", [P, NT, S])
        attT = [sb(f"attT{p}", [P, NT, S], F32R) for p in "hl"]
        up = [sb(f"up{p}", [P, NT, P], F32R) for p in "hl"]
        low = [sb(f"low{p}", [P, NT, P], F32R) for p in "hl"]
        hlr = [sb(f"hlr{p}", [P, NT, 2, D], F32R) for p in "hl"]
        self_part = sb("self_part", [P, NT, D])
        mixed = sb("mixed", [P, NT, D])
        normed = sb("normed", [P, NT, D])
        diag_tmp = sb("diag_tmp", [P, P])
        y_in = sb("y_in", [P, NT, D])
        res = sb("res", [P, NT, D])
        bias_adj = sb("bias_adj", [P, NT, S])
        qk_hi = sb("qk_hi", [P, 2, NC, S], F32R)
        qk_lo = sb("qk_lo", [P, 2, NC, S], F32R)
        q_st = sb("q_st", [P, NH, S], F32R)
        k_st = sb("k_st", [P, NH, S], F32R)
        v_parts = sb("v_parts", [P, NT, NH, VP, HD], BF16)
        v_rest = sb("v_rest", [P, NT, D])
        neg_adj = v_rest[:, :, 0:S]
        masked = sb("masked", [P, NT, S])
        prob = sb("prob", [P, 2, NT, S])
        pT_hi = sb("pT_hi", [P, 2, NT, S], F16)
        pT_lo = sb("pT_lo", [P, 2, NT, S], F16)
        result = sb("result", [P, NT, D])
        att = result[:, :, :].rearrange("p i (h d) -> p i h d", h=NH)
        negmax = sb("negmax", [P, NT])
        ubias = sb("ubias", [P, NT])
        zsum = sb("zsum", [P, NT])
        ssum = sb("ssum", [P, NT])
        diag = sb("diag", [P, NT])
        inv_s = sb("inv_s", [P, NT])
        hmin = sb("hmin", [P, NT, NH])
        hsum = sb("hsum", [P, NT, NH])
        hinv = sb("hinv", [P, NT, NH])
        norms = ("a", "b", "y", "c")
        stats = {k: sb(f"stats_{k}", [P, NT, 6]) for k in norms}
        mv = {k: sb(f"mv_{k}", [P, NT, 2]) for k in norms}
        var = {k: sb(f"var_{k}", [P, NT]) for k in norms}
        lnv = {k: sb(f"lnv_{k}", [P, NT]) for k in norms}
        y0 = {k: sb(f"y0_{k}", [P, NT]) for k in norms}
        tmp = {k: sb(f"tmp_{k}", [P, NT]) for k in norms}
        rstd = {k: sb(f"rstd_{k}", [P, NT]) for k in norms}

        staging = [buf[:, i, :] for buf in (normed, y_in, res, result, v_rest) for i in range(NT)][:9]

        bank_w = [bank("bank_w0"), bank("bank_w1")]
        bank_u = bank("bank_u")
        bank_t = bank("bank_t")
        bank_m = bank("bank_m")
        bank_s = bank("bank_s")
        bank_p = bank("bank_p")
        bank_o = bank("bank_o")

        s_setup = sem("s_setup")
        s_const = sem("s_const")
        s_stage = sem("s_stage")
        s_split = sem("s_split")
        s_pool_c = sem("s_pool_c")
        s_xa, s_xb = sem("s_xa"), sem("s_xb")
        s_adj = {k: sem(f"s_adj_{k}") for k in "abc"}
        s_tx_pe, s_tx_hi, s_tx_lo = sem("s_tx_pe"), sem("s_tx_hi"), sem("s_tx_lo")
        s_th_pe, s_th_f, s_th_lo = sem("s_th_pe"), sem("s_th_f"), sem("s_th_lo")
        s_ty_pe, s_ty_hi, s_ty_lo = sem("s_ty_pe"), sem("s_ty_hi"), sem("s_ty_lo")
        s_u, s_ub, s_exp, s_em = sem("s_u"), sem("s_ub"), sem("s_exp"), sem("s_em")
        s_proj, s_proj_hi, s_proj_rd = sem("s_proj"), sem("s_proj_hi"), sem("s_proj_rd")
        s_at, s_at_hi, s_at_lo, s_cut = sem("s_at"), sem("s_at_hi"), sem("s_at_lo"), sem("s_cut")
        s_mix, s_mix_rd = sem("s_mix"), sem("s_mix_rd")
        s_var = {k: sem(f"s_var_{k}") for k in norms}
        s_ln = {k: sem(f"s_ln_{k}") for k in norms}
        s_y0 = {k: sem(f"s_y0_{k}") for k in norms}
        s_self, s_diag = sem("s_self"), sem("s_diag")
        s_h1, s_resid, s_y = sem("s_h1"), sem("s_resid"), sem("s_y")
        s_res, s_badj = sem("s_res"), sem("s_badj")
        s_qk, s_qk_hi, s_qk_lo = sem("s_qk"), sem("s_qk_hi"), sem("s_qk_lo")
        s_stack = {k: sem(f"s_stack_{k}") for k in "qk"}
        s_v, s_v_hi, s_v_rd, s_v_all, s_v_mid = sem("s_v"), sem("s_v_hi"), sem("s_v_rd"), sem("s_v_all"), sem("s_v_mid")
        s_sc, s_msk, s_prob = sem("s_sc"), sem("s_msk"), sem("s_prob")
        s_pt, s_pt_hi, s_pt_lo = sem("s_pt"), sem("s_pt_hi"), sem("s_pt_lo")
        s_pv, s_att = sem("s_pv"), sem("s_att")
        s_out_ok, s_out = sem("s_out_ok"), sem("s_out")
        s_apart = sem("s_apart")
        s_dve, s_pool = sem("s_dve"), sem("s_pool")

        def wait(eng, s, count):
            if not (isinstance(count, int) and count <= 0):
                eng.wait_ge(s, count)

        def apart(eng):
            eng.sem_inc(s_apart, 1)

        STACKED = 16 * SLOTS * HPG

        def layer_a(t):
            return 2 * t

        def layer_b(t):
            return 2 * t - 1

        def run(steps, todo, t):
            for name, k in todo:
                if name in steps:
                    steps[name](t, k)

        def pipeline(eng, body):
            body(0, schedule(True, False, False, False))
            body(1, schedule(True, True, False, False))
            body(2, schedule(True, True, True, False))
            with eng.Fori(3, NB) as t:
                body(t, schedule(True, True, True, True))
            body(NB, schedule(False, True, True, True))
            body(NB + 1, schedule(False, False, True, True))
            body(NB + 2, schedule(False, False, False, True))

        block = ctx.enter_context(nc.Block())

        @block.sync
        def _(sp):
            for l in range(LAYERS):
                for m, b in enumerate((bl, bs, br)):
                    for half in range(2):
                        r = 64 * l + 32 * half
                        sp.dma_start(self_part[r:r + 1, :, :].rearrange("p i d -> p (i d)")[:, 0:D] if m == 0 else
                                     (self_part[r:r + 1, 1, :] if m == 1 else mixed[r:r + 1, 0, :]),
                                     b[l:l + 1, :]).then_inc(s_const, 16)
            sp.dma_start(q_bias[:, :], bq.rearrange("(g p) -> p g", p=P), allow_slow_non_contiguous=True).then_inc(s_const, 16)
            sp.dma_start(k_bias[:, :], bk.rearrange("(g p) -> p g", p=P), allow_slow_non_contiguous=True).then_inc(s_const, 16)
            sp.dma_start(g1_col[:, :], ln_w[0, :].rearrange("(g p) -> p g", p=P), allow_slow_non_contiguous=True).then_inc(s_const, 16)
            sp.dma_start(b1_col[:, :], ln_b[0, :].rearrange("(g p) -> p g", p=P), allow_slow_non_contiguous=True).then_inc(s_const, 16)
            sp.dma_start(v_bias[:, :], bv.partition_broadcast(P)).then_inc(s_const, 16)
            sp.dma_start(g2_row[:, :], ln_w[1, :].partition_broadcast(P)).then_inc(s_const, 16)
            sp.dma_start(b2_row[:, :], ln_b[1, :].partition_broadcast(P)).then_inc(s_const, 16)
            sp.dma_start(beta_col[:, :], beta.partition_broadcast(P)).then_inc(s_const, 16)

            sp.wait_ge(s_setup, 1)

            def stack(c, which):
                side = "qk".index(which)
                wait(sp, s_qk_lo, NC * (2 * c + side + 1))
                apart(sp)
                for slot in range(SLOTS):
                    part = (qk_hi, (qk_lo, qk_hi)[side], (qk_hi, qk_lo)[side])[slot]
                    for r in range(HPG):
                        sp.dma_start((q_st, k_st)[side][slot * HD:(slot + 1) * HD, r::HPG, :].bitcast(F32),
                                     part[r * HD:(r + 1) * HD, side, :, :].bitcast(F32)).then_inc(s_stack[which], 16)

            def body(t, todo):
                names = [n for n, _ in todo]
                in_a, in_b, in_c = "a_scores" in names, "b_scores" in names, "scores" in names
                if in_c:
                    wait(sp, s_em, 2 * (layer_a(t - 1) + 1) if not (isinstance(t, int) and t > NB)
                         else 2 * (layer_b(t - 1) + 1))
                    apart(sp)
                    sp.dma_start(adj_in[:, :, :], adj_v[t - 2]).then_inc(s_adj["c"], 16)
                if in_a:
                    wait(sp, s_resid, (t - 1) * NT)
                    if isinstance(t, int) and t == 1:
                        sp.wait_ge(s_tx_pe, NC)
                    apart(sp)
                    sp.dma_start(x_in[:, :, :], x_v[t]).then_inc(s_xa, 16)
                if in_c:
                    stack(t - 2, "q")
                if in_b:
                    if in_c:
                        wait(sp, s_badj, t - 1)
                    else:
                        wait(sp, s_em, 2 * (layer_a(t - 1) + 1))
                    apart(sp)
                    sp.dma_start(adj_in[:, :, :], adj_v[t - 1]).then_inc(s_adj["b"], 16)
                if in_c:
                    stack(t - 2, "k")
                if in_b:
                    if in_a:
                        wait(sp, s_tx_pe, NC * (t + 1))
                    else:
                        wait(sp, s_resid, (t - 1) * NT)
                    apart(sp)
                    sp.dma_start(x_in[:, :, :], x_v[t - 1]).then_inc(s_xb, 16)
                if in_a:
                    if in_b:
                        wait(sp, s_em, 2 * (layer_b(t) + 1))
                    apart(sp)
                    sp.dma_start(adj_in[:, :, :], adj_v[t]).then_inc(s_adj["a"], 16)

            pipeline(sp, body)
            sp.wait_ge(s_out, 16 * NB)

        @block.tensor
        def _(pe):
            def mm(dst, lhsT, rhs, start, stop):
                return nc.tensor.matmul(dst, lhsT, rhs, start=start, stop=stop)

            def turn_x(t, k):
                pe.wait_ge(s_xa, 16 * (t + 1))
                wait(pe, s_th_lo, NC * t) if k == 0 else None
                wait(pe, s_tx_lo, NC * t + k)
                for i in range(NT):
                    last = nc.tensor.transpose(bank_t[:, i * P:(i + 1) * P], x_in[:, i, k * P:(k + 1) * P], ident[:, :])
                last.then_inc(s_tx_pe, 1)

            def turn_h(t, k):
                pe.wait_ge(s_h1, NT * t)
                if k == 0:
                    wait(pe, s_ty_lo, NC * (t - 1))
                    pe.wait_ge(s_tx_lo, NC * t)
                wait(pe, s_th_lo, NC * (t - 1) + k)
                for i in range(NT):
                    last = nc.tensor.transpose(bank_t[:, i * P:(i + 1) * P], normed[:, i, k * P:(k + 1) * P], ident[:, :])
                last.then_inc(s_th_pe, 1)

            def turn_y(t, k):
                pe.wait_ge(s_y, NT * t)
                if k == 0:
                    pe.wait_ge(s_th_lo, NC * t)
                    if not (isinstance(t, int) and t == NB):
                        pe.wait_ge(s_tx_lo, NC * (t + 1))
                wait(pe, s_ty_lo, NC * (t - 1) + k)
                for i in range(NT):
                    last = nc.tensor.transpose(bank_t[:, i * P:(i + 1) * P], y_in[:, i, k * P:(k + 1) * P], ident[:, :])
                last.then_inc(s_ty_pe, 1)

            def graph_scores(n, hT, ready):
                ready()
                wait(pe, s_at_lo, n)
                for i in range(NT):
                    for c in range(NC):
                        for a, b in PARTS:
                            last = mm(bank_u[:, i * S:(i + 1) * S], hT[a][:, c, i * P:(i + 1) * P], hT[b][:, c, :],
                                      c == 0 and (a, b) == PARTS[0], c == NC - 1 and (a, b) == PARTS[-1])
                last.then_inc(s_u, 1)

            def a_scores(t, _k):
                graph_scores(layer_a(t), hT_ac, lambda: pe.wait_ge(s_tx_lo, NC * (t + 1)))

            def b_scores(t, _k):
                graph_scores(layer_b(t), hT_b, lambda: pe.wait_ge(s_th_lo, NC * t))

            def projection(n, layer, hT, j):
                m, i = j // 2, j % 2
                if j in (2, 3):
                    pe.wait_ge(s_proj_rd, 4 * n + j - 1)
                if j >= 4:
                    pe.wait_ge(s_self, 2 * n + j - 3)
                for c in range(NC):
                    for a, b in PARTS:
                        mm(bank_w[i][:, 0:D], hT[a][:, c, i * P:(i + 1) * P], w_graph[layer][b][:, c, m, :],
                           c == 0 and (a, b) == PARTS[0], False)
                mm(bank_w[i][:, 0:D], pick_bias[layer][:, :], bias_rows[:, m, :], False, True).then_inc(s_proj, 1)

            def a_proj(t, j):
                if j < 2:
                    wait(pe, s_proj_rd, 4 * layer_a(t) - 1 + j)
                projection(layer_a(t), 0, hT_ac, j)

            def b_proj(t, j):
                if j < 2:
                    wait(pe, s_proj_rd, 4 * layer_b(t) - 1 + j)
                    wait(pe, s_v_rd, NT * (t - 1) - 1 + j)
                projection(layer_b(t), 1, hT_b, j)

            def graph_turn(n):
                pe.wait_ge(s_em, 2 * (n + 1))
                for j in range(NT):
                    for i in range(NT):
                        last = nc.tensor.transpose(bank_u[:, j * S + i * P:j * S + (i + 1) * P],
                                                   expu[:, i, j * P:(j + 1) * P], ident[:, :])
                last.then_inc(s_at, 1)

            def mix(n, i):
                pe.wait_ge(s_cut, n + 1)
                pe.wait_ge(s_proj_rd, 4 * (n + 1))
                wait(pe, s_mix_rd, 2 * n + i)
                other = 1 - i
                terms = ([(up, i, None, i, 0)], [(low, i, None, i, 1)],
                         [(attT, other, i, other, 0 if i == 0 else 1)])
                terms = [x[0] for x in terms]
                count = 0
                for src, jb, ib, j, side in terms:
                    for a, b in PARTS:
                        w = src[a][:, jb, :] if ib is None else src[a][:, jb, ib * P:(ib + 1) * P]
                        last = mm(bank_m[:, 0:D], w, hlr[b][:, j, side, :], count == 0, count == 8)
                        count += 1
                last.then_inc(s_mix, 1)

            def qk(t, side, g):
                s, j = t - 2, NC * side + g
                if j == 0:
                    pe.wait_ge(s_ty_lo, NC * (t - 1))
                if j < 2:
                    last_layer = layer_b(t - 1) if isinstance(t, int) and t == NB + 1 else layer_a(t - 1)
                    pe.wait_ge(s_proj_rd, 4 * last_layer + 3 + j)
                else:
                    pe.wait_ge(s_qk_lo, 6 * s + j - 1)
                for c in range(NC):
                    for a, b in PARTS:
                        last = mm(bank_w[j % 2][:, 0:S], w_qkv[a][:, c, side, g * P:(g + 1) * P], hT_ac[b][:, c, :],
                                  c == 0 and (a, b) == PARTS[0], c == NC - 1 and (a, b) == PARTS[-1])
                last.then_inc(s_qk, 1)

            def v(t, i):
                s = t - 2
                pe.wait_ge(s_qk_lo, 6 * s + 5 + i)
                for c in range(NC):
                    for a, b in PARTS:
                        last = mm(bank_w[i][:, 0:D], hT_ac[a][:, c, i * P:(i + 1) * P], w_qkv[b][:, c, 2, :],
                                  c == 0 and (a, b) == PARTS[0], c == NC - 1 and (a, b) == PARTS[-1])
                last.then_inc(s_v, 1)

            def scores(t, h):
                s = t - 2
                if h == 0:
                    pe.wait_ge(s_stack["q"], STACKED * (s + 1))
                    pe.wait_ge(s_stack["k"], STACKED * (s + 1))
                wait(pe, s_msk, NT * (NH * s + h))
                for i in range(NT):
                    last = mm(bank_s[:, i * S:(i + 1) * S], q_st[0:SLOTS * HD, h, i * P:(i + 1) * P],
                              k_st[0:SLOTS * HD, h, :], True, True)
                last.then_inc(s_sc, 1)

            def weights(t, h):
                s = t - 2
                pe.wait_ge(s_prob, NT * (NH * s + h + 1))
                wait(pe, s_pt_lo, NH * s + h)
                for j in range(NT):
                    for i in range(NT):
                        last = nc.tensor.transpose(bank_p[:, j * S + i * P:j * S + (i + 1) * P],
                                                   prob[:, h % 2, i, j * P:(j + 1) * P], ident[:, :])
                last.then_inc(s_pt, 1)

            def attend(t, h):
                s = t - 2
                pe.wait_ge(s_pt_lo, NH * s + h + 1)
                if h == 0:
                    pe.wait_ge(s_v_all, NT * (s + 1))
                if h % 2 == 0:
                    wait(pe, s_att, (NH * s + h) // 2 if isinstance(s, int) else NH // 2 * s + h // 2)
                for i in range(NT):
                    at = (NT * (h % 2) + i) * VP * HD
                    for j in range(NT):
                        vp = v_parts[:, j, h, :, :].rearrange("p a d -> p (a d)")
                        mm(bank_o[:, at:at + VP * HD], pT_hi[:, h % 2, j, i * P:(i + 1) * P], vp, j == 0, False)
                        last = mm(bank_o[:, at:at + 2 * HD], pT_lo[:, h % 2, j, i * P:(i + 1) * P], vp[:, 0:2 * HD],
                                  False, j == NT - 1)
                last.then_inc(s_pv, 1)

            steps = {
                "turn_x": turn_x, "turn_h": turn_h, "turn_y": turn_y,
                "a_scores": a_scores, "b_scores": b_scores, "a_proj": a_proj, "b_proj": b_proj,
                "a_turn": lambda t, k: graph_turn(layer_a(t)), "b_turn": lambda t, k: graph_turn(layer_b(t)),
                "a_mix": lambda t, k: mix(layer_a(t), k), "b_mix": lambda t, k: mix(layer_b(t), k),
                "q": lambda t, k: qk(t, 0, k), "k": lambda t, k: qk(t, 1, k), "v": v, "scores": scores, "weights": weights, "attend": attend,
            }
            pe.wait_ge(s_setup, 1)
            pipeline(pe, lambda t, todo: run(steps, todo, t))

        @block.scalar
        def _(act):
            nc.scalar.preload_act_table_set("natural_log_exp_and_others")

            for n, (mats, l) in enumerate((((wl, ws, wr), 0), ((wl, ws, wr), 1), ((wq, wk, wv), None))):
                wait(act, s_split, 18 * n)
                for m, w in enumerate(mats):
                    for c in range(NC):
                        src = (w[l] if l is not None else w)[c * P:(c + 1) * P, :]
                        act.dma_start(staging[NC * m + c], src).then_inc(s_stage, 16)

            def turn_x(t, k):
                act.wait_ge(s_tx_pe, NC * t + k + 1)
                if k == 0:
                    wait(act, s_v, NT * (t - 1))
                nc.scalar.activation(hT_ac[0][:, k, :], bank_t[:, 0:S], ACT.Copy).then_inc(s_tx_hi, 1)

            def turn_y(t, k):
                act.wait_ge(s_ty_pe, NC * (t - 1) + k + 1)
                if k == 0 and not (isinstance(t, int) and t == NB):
                    act.wait_ge(s_proj, 6 * layer_a(t) + 6)
                nc.scalar.activation(hT_ac[0][:, k, :], bank_t[:, 0:S], ACT.Copy).then_inc(s_ty_hi, 1)

            def turn_h(t, k):
                act.wait_ge(s_th_pe, NC * (t - 1) + k + 1)
                nc.scalar.activation(mixed[:, 0, 0:S] if k == 0 else (mixed[:, 1, 0:S] if k == 1 else self_part[:, 0, 0:S]),
                                     bank_t[:, 0:S], ACT.Relu, bias=b1_col[:, k:k + 1],
                                     scale=g1_col[:, k:k + 1]).then_inc(s_th_f, 1)

            def graph_exp(n):
                act.wait_ge(s_ub, n + 1)
                wait(act, s_at, n)
                for i in range(NT):
                    nc.scalar.activation(expu[:, i, :], bank_u[:, i * S:(i + 1) * S], ACT.Exp, bias=ubias[:, i:i + 1],
                                         scale=TEMPER, accum_out=zsum[:, i:i + 1]).then_inc(s_exp, 1)

            def proj_hi(n, j):
                m, i = j // 2, j % 2
                act.wait_ge(s_proj, 6 * n + j + 1)
                if m == 1:
                    act.wait_ge(s_diag, n + 1)
                    wait(act, s_mix_rd, 2 * n)
                    nc.scalar.activation(self_part[:, i, :], bank_w[i][:, 0:D], ACT.Copy,
                                         scale=diag[:, i:i + 1]).then_inc(s_self, 1)
                else:
                    if j == 0:
                        wait(act, s_mix, 2 * n)
                    nc.scalar.activation(hlr[0][:, i, m // 2, :], bank_w[i][:, 0:D], ACT.Copy).then_inc(s_proj_hi, 1)

            def graph_turn(n):
                act.wait_ge(s_at, n + 1)
                wait(act, s_mix, 2 * n)
                wait(act, s_cut, n)
                nc.scalar.activation(attT[0][:, :, :].rearrange("p j i -> p (j i)"), bank_u[:, :], ACT.Copy).then_inc(s_at_hi, 1)

            def root(k, index):
                act.wait_ge(s_var[k], index + 1)
                nc.scalar.activation(lnv[k][:, :], var[k][:, :], ACT.Ln).then_inc(s_ln[k], 1)
                act.wait_ge(s_ln[k], index + 1)
                nc.scalar.activation(y0[k][:, :], lnv[k][:, :], ACT.Exp, scale=-0.5).then_inc(s_y0[k], 1)

            def c_norm(t, _k):
                root("c", t - 3)

            def c_apply(t, _k):
                act.wait_ge(s_out_ok, (t - 2) * NT)
                act.dma_start(out_v[t - 3], result[:, :, :]).then_inc(s_out, 16)

            def qk(t, side, g):
                s, j = t - 2, NC * side + g
                act.wait_ge(s_qk, 6 * s + j + 1)
                wait(act, s_stack["qk"[side]], STACKED * s)
                nc.scalar.activation(qk_hi[:, side, g, :], bank_w[j % 2][:, 0:S], ACT.Identity,
                                     bias=(q_bias, k_bias)[side][:, g:g + 1]).then_inc(s_qk_hi, 1)

            def v(t, i):
                s = t - 2
                act.wait_ge(s_v, NT * s + i + 1)
                if i == 0:
                    wait(act, s_pv, NH * s)
                nc.scalar.activation(v_parts[:, i, :, 0, :], bank_w[i][:, 0:D].rearrange("p (h d) -> p h d", h=NH),
                                     ACT.Copy).then_inc(s_v_hi, 1)

            def scores(t, h):
                s = t - 2
                wait(act, s_pt, NH * s + max(h - 1, 0))
                for i in range(NT):
                    act.wait_ge(s_msk, NT * (NH * s + h) + i + 1)
                    nc.scalar.activation(prob[:, h % 2, i, :], masked[:, i, :], ACT.Exp, bias=hmin[:, i, h:h + 1],
                                         scale=-1.0, accum_out=hsum[:, i, h:h + 1]).then_inc(s_prob, 1)

            def weights(t, h):
                s = t - 2
                act.wait_ge(s_pt, NH * s + h + 1)
                wait(act, s_pv, NH * s + max(h - 1, 0))
                nc.scalar.activation(pT_hi[:, h % 2, :, :].rearrange("p j i -> p (j i)"), bank_p[:, :], ACT.Copy).then_inc(s_pt_hi, 1)

            steps = {
                "turn_x": turn_x, "turn_h": turn_h, "turn_y": turn_y,
                "a_scores": lambda t, k: graph_exp(layer_a(t)), "b_scores": lambda t, k: graph_exp(layer_b(t)),
                "a_proj": lambda t, k: proj_hi(layer_a(t), k), "b_proj": lambda t, k: proj_hi(layer_b(t), k),
                "a_turn": lambda t, k: graph_turn(layer_a(t)), "b_turn": lambda t, k: graph_turn(layer_b(t)),
                "a_norm": lambda t, k: root("a", t), "b_norm": lambda t, k: root("b", t - 1),
                "b_apply": lambda t, k: root("y", t - 1), "c_norm": c_norm, "c_apply": c_apply,
                "q": lambda t, k: qk(t, 0, k), "k": lambda t, k: qk(t, 1, k), "v": v, "scores": scores, "weights": weights,
            }
            pipeline(act, lambda t, todo: run(steps, todo, t))

        @block.vector
        def _(dve):
            ve = nc.vector
            links = [0, 0]

            def link(ins):
                ins.then_inc(s_dve, 1)
                links[1] += 1
                dve.wait_ge(s_dve, links[0] + links[1])

            for n, w in enumerate((w_graph[0], w_graph[1], w_qkv)):
                dve.wait_ge(s_stage, 16 * 9 * (n + 1))
                for k in range(9):
                    m, c = k // NC, k % NC
                    ve.tensor_copy(w[0][:, c, m, :], staging[k]).then_inc(s_split, 1)
                    dve.wait_ge(s_split, 18 * n + 2 * k + 1)
                    ve.tensor_tensor(w[1][:, c, m, :], staging[k], w[0][:, c, m, :], ALU.subtract).then_inc(s_split, 1)
            dve.wait_ge(s_pool_c, 8)
            dve.wait_ge(s_const, 16 * 20)
            srcs = (self_part[:, 0, :], self_part[:, 1, :], mixed[:, 0, :])
            for l in range(LAYERS):
                for half in range(2):
                    r = 64 * l + 32 * half
                    link(ve.memset(pick_bias[l][r:r + 1, :].bitcast(F32), 1.0))
            for m in range(3):
                for l in range(LAYERS):
                    r = 64 * l
                    link(ve.tensor_copy(bias_rows[r:r + 1, m, :], srcs[m][r:r + 1, :]))
                    link(ve.tensor_copy(bias_rows[r + 32:r + 33, m, :], srcs[m][r + 32:r + 33, :]))
                    link(ve.tensor_tensor(bias_rows[r + 32:r + 33, m, :], srcs[m][r + 32:r + 33, :],
                                          bias_rows[r + 32:r + 33, m, :], ALU.subtract))
            dve.wait_ge(s_split, 54)
            ve.tensor_scalar(beta_col[:, :], beta_col[:, :], 1.0 / SCALE, None, ALU.mult).then_inc(s_setup, 1)
            dve.wait_ge(s_setup, 1)

            def turn_x(t, k):
                dve.wait_ge(s_tx_hi, NC * t + k + 1)
                ve.tensor_tensor(hT_ac[1][:, k, :], bank_t[:, 0:S], hT_ac[0][:, k, :], ALU.subtract).then_inc(s_tx_lo, 1)

            def turn_y(t, k):
                dve.wait_ge(s_ty_hi, NC * (t - 1) + k + 1)
                ve.tensor_tensor(hT_ac[1][:, k, :], bank_t[:, 0:S], hT_ac[0][:, k, :], ALU.subtract).then_inc(s_ty_lo, 1)

            def turn_h(t, k):
                dve.wait_ge(s_th_f, NC * (t - 1) + k + 1)
                f = mixed[:, 0, 0:S] if k == 0 else (mixed[:, 1, 0:S] if k == 1 else self_part[:, 0, 0:S])
                link(ve.tensor_copy(hT_b[0][:, k, :], f))
                ve.tensor_tensor(hT_b[1][:, k, :], f, hT_b[0][:, k, :], ALU.subtract).then_inc(s_th_lo, 1)

            def graph_scores(n):
                dve.wait_ge(s_u, n + 1)
                link(ve.tensor_reduce(negmax[:, :], bank_u[:, :].rearrange("p (i j) -> p i j", i=NT), AX.X, ALU.max, negate=True))
                ve.tensor_scalar(ubias[:, :], negmax[:, :], TEMPER, None, ALU.mult).then_inc(s_ub, 1)

            def graph_mask(n, s_loaded, count):
                wait(dve, s_self, 2 * n)
                dve.wait_ge(s_loaded, count)
                for i in range(NT):
                    dve.wait_ge(s_exp, 2 * n + i + 1)
                    ve.scalar_tensor_tensor(expu[:, i, :], expu[:, i, :], 1.0, adj_in[:, i, :], ALU.mult, ALU.mult,
                                            accum_out=ssum[:, i:i + 1]).then_inc(s_em, 1)
                dve.wait_ge(s_em, 2 * (n + 1))
                for i in range(NT):
                    ins = ve.scalar_tensor_tensor(diag_tmp[:, :], expu[:, i, i * P:(i + 1) * P], 1.0, ident[:, :],
                                                  ALU.mult, ALU.mult, accum_out=diag[:, i:i + 1])
                    if i == 0:
                        link(ins)
                ins.then_inc(s_diag, 1)
                link(ve.scalar_tensor_tensor(inv_s[:, :], zsum[:, :], EPS_ATTN, ssum[:, :], ALU.mult, ALU.add))
                link(ve.reciprocal(inv_s[:, :], inv_s[:, :]))

            def projection(n, j):
                m, i = j // 2, j % 2
                if m != 1:
                    dve.wait_ge(s_proj_hi, 4 * n + (j if m == 0 else j - 2) + 1)
                    ve.tensor_tensor(hlr[1][:, i, m // 2, :], bank_w[i][:, 0:D], hlr[0][:, i, m // 2, :],
                                     ALU.subtract).then_inc(s_proj_rd, 1)

            def graph_turn(n):
                dve.wait_ge(s_at_hi, n + 1)
                ve.tensor_tensor(attT[1][:, :, :].rearrange("p j i -> p (j i)"), bank_u[:, :],
                                 attT[0][:, :, :].rearrange("p j i -> p (j i)"), ALU.subtract).then_inc(s_at_lo, 1)

            def mix(n, i, k):
                dve.wait_ge(s_mix, 2 * n + i + 1)
                dve.wait_ge(s_self, 2 * (n + 1))
                ve.tensor_tensor(mixed[:, i, :], bank_m[:, 0:D], self_part[:, i, :], ALU.add).then_inc(s_mix_rd, 1)
                dve.wait_ge(s_mix_rd, 2 * n + i + 1)
                link(ve.bn_stats(stats[k][:, i, :], mixed[:, i, :]))
                apart(dve)
                link(ve.bn_aggr(mv[k][:, i, :], stats[k][:, i, :]))

            def refine(k, index):
                dve.wait_ge(s_y0[k], index + 1)
                link(ve.tensor_tensor(tmp[k][:, :], y0[k][:, :], y0[k][:, :], ALU.mult))
                link(ve.tensor_tensor(tmp[k][:, :], tmp[k][:, :], var[k][:, :], ALU.mult))
                link(ve.tensor_scalar(tmp[k][:, :], tmp[k][:, :], -0.5, 1.5, ALU.mult, ALU.add))
                link(ve.tensor_tensor(rstd[k][:, :], tmp[k][:, :], y0[k][:, :], ALU.mult))

            def graph_norm(k):
                link(ve.tensor_tensor(tmp[k][:, :], mv[k][:, :, 1], inv_s[:, :], ALU.mult))
                link(ve.tensor_tensor(tmp[k][:, :], tmp[k][:, :], inv_s[:, :], ALU.mult))
                ve.tensor_scalar(var[k][:, :], tmp[k][:, :], EPS_GRAPH, None, ALU.add).then_inc(s_var[k], 1)

            def a_apply(t, _k):
                refine("a", t)
                link(ve.tensor_tensor(rstd["a"][:, :], rstd["a"][:, :], inv_s[:, :], ALU.mult))
                for i in range(NT):
                    ve.tensor_scalar(normed[:, i, :], mixed[:, i, :], mv["a"][:, i, 0:1], rstd["a"][:, i:i + 1],
                                     ALU.subtract, ALU.mult).then_inc(s_h1, 1)

            def b_apply(t, _k):
                refine("b", t - 1)
                link(ve.tensor_tensor(rstd["b"][:, :], rstd["b"][:, :], inv_s[:, :], ALU.mult))
                dve.wait_ge(s_xb, 16 * t)
                for i in range(NT):
                    link(ve.scalar_tensor_tensor(normed[:, i, :], mixed[:, i, :], mv["b"][:, i, 0:1], g2_row[:, :],
                                                 ALU.subtract, ALU.mult))
                    link(ve.scalar_tensor_tensor(normed[:, i, :], normed[:, i, :], rstd["b"][:, i:i + 1], b2_row[:, :],
                                                 ALU.mult, ALU.add))
                    ve.scalar_tensor_tensor(normed[:, i, :], normed[:, i, :], 0.0, x_in[:, i, :],
                                            ALU.max, ALU.add).then_inc(s_resid, 1)
                    dve.wait_ge(s_resid, NT * (t - 1) + i + 1)
                    link(ve.bn_stats(stats["y"][:, i, :], normed[:, i, :]))
                    apart(dve)
                    link(ve.bn_aggr(mv["y"][:, i, :], stats["y"][:, i, :]))
                ve.tensor_scalar(var["y"][:, :], mv["y"][:, :, 1], EPS_NORM, None, ALU.add).then_inc(s_var["y"], 1)

            def b_out(t, _k):
                refine("y", t - 1)
                if not (isinstance(t, int) and t == 1):
                    dve.wait_ge(s_res, t - 1)
                for i in range(NT):
                    ve.tensor_scalar(y_in[:, i, :], normed[:, i, :], mv["y"][:, i, 0:1], rstd["y"][:, i:i + 1],
                                     ALU.subtract, ALU.mult).then_inc(s_y, 1)

            def qk(t, side, g):
                s, j = t - 2, NC * side + g
                dve.wait_ge(s_qk_hi, 6 * s + j + 1)
                ve.scalar_tensor_tensor(qk_lo[:, side, g, :], bank_w[j % 2][:, 0:S],
                                        (q_bias, k_bias)[side][:, g:g + 1], qk_hi[:, side, g, :],
                                        ALU.add, ALU.subtract).then_inc(s_qk_lo, 1)

            def v(t, i):
                s = t - 2
                dve.wait_ge(s_v_hi, NT * s + i + 1)
                if i == 0:
                    dve.wait_ge(s_badj, s + 1)
                ve.tensor_tensor(v_rest[:, i, :].rearrange("p (h d) -> p h d", h=NH),
                                 bank_w[i][:, 0:D].rearrange("p (h d) -> p h d", h=NH),
                                 v_parts[:, i, :, 0, :], ALU.subtract).then_inc(s_v_rd, 1)

            def scores(t, h):
                s = t - 2
                dve.wait_ge(s_sc, NH * s + h + 1)
                if h == 0:
                    dve.wait_ge(s_badj, s + 1)
                wait(dve, s_prob, NT * (NH * s + h))
                apart(dve)
                for i in range(NT):
                    ve.tensor_tensor_reduce(masked[:, i, :], bank_s[:, i * S:(i + 1) * S], bias_adj[:, i, :],
                                            -SCALE, BIG, ALU.add, ALU.min, hmin[:, i, h:h + 1]).then_inc(s_msk, 1)

            def weights(t, h):
                s = t - 2
                dve.wait_ge(s_pt_hi, NH * s + h + 1)
                ve.tensor_tensor(pT_lo[:, h % 2, :, :].rearrange("p j i -> p (j i)"), bank_p[:, :],
                                 pT_hi[:, h % 2, :, :].rearrange("p j i -> p (j i)"), ALU.subtract).then_inc(s_pt_lo, 1)

            def attend(t, h):
                if h % 2 == 1:
                    s = t - 2
                    if h == 1:
                        wait(dve, s_out, 16 * s)
                    dve.wait_ge(s_pv, NH * s + h + 1)
                    for k in range(2):
                        at = k * NT * VP * HD
                        ins = ve.tensor_reduce(att[:, :, h - 1 + k, :],
                                               bank_o[:, at:at + NT * VP * HD].rearrange("p (i a d) -> p i d a", i=NT, a=VP),
                                               AX.X, ALU.add)
                        if k == 0:
                            link(ins)
                    ins.then_inc(s_att, 1)

            def c_sum(t, _k):
                s = t - 3
                dve.wait_ge(s_prob, NT * NH * (s + 1))
                link(ve.reciprocal(hinv[:, :, :], hsum[:, :, :]))
                dve.wait_ge(s_att, NH // 2 * (s + 1))
                dve.wait_ge(s_res, s + 1)
                for i in range(NT):
                    link(ve.tensor_tensor(att[:, i, :, :], att[:, i, :, :],
                                          hinv[:, i, :].unsqueeze(2).to_broadcast([P, NH, HD]), ALU.mult))
                    link(ve.tensor_tensor(result[:, i, :], att[:, i, :, :].rearrange("p h d -> p (h d)"), res[:, i, :], ALU.add))
                    link(ve.bn_stats(stats["c"][:, i, :], result[:, i, :]))
                    apart(dve)
                    link(ve.bn_aggr(mv["c"][:, i, :], stats["c"][:, i, :]))
                ve.tensor_scalar(var["c"][:, :], mv["c"][:, :, 1], EPS_NORM, None, ALU.add).then_inc(s_var["c"], 1)

            def c_apply(t, _k):
                refine("c", t - 3)
                for i in range(NT):
                    ve.tensor_scalar(result[:, i, :], result[:, i, :], mv["c"][:, i, 0:1], rstd["c"][:, i:i + 1],
                                     ALU.subtract, ALU.mult).then_inc(s_out_ok, 1)

            def a_mask(t, _k):
                graph_mask(layer_a(t), s_adj["a"], 16 * (t + 1))

            def b_mask(t, _k):
                graph_mask(layer_b(t), s_adj["b"], 16 * t)

            steps = {
                "turn_x": turn_x, "turn_h": turn_h, "turn_y": turn_y,
                "a_scores": lambda t, k: graph_scores(layer_a(t)), "b_scores": lambda t, k: graph_scores(layer_b(t)),
                "a_mask": a_mask, "b_mask": b_mask,
                "a_proj": lambda t, k: projection(layer_a(t), k), "b_proj": lambda t, k: projection(layer_b(t), k),
                "a_turn": lambda t, k: graph_turn(layer_a(t)), "b_turn": lambda t, k: graph_turn(layer_b(t)),
                "a_mix": lambda t, k: mix(layer_a(t), k, "a"), "b_mix": lambda t, k: mix(layer_b(t), k, "b"),
                "a_norm": lambda t, k: graph_norm("a"), "b_norm": lambda t, k: graph_norm("b"),
                "a_apply": a_apply, "b_apply": b_apply, "b_out": b_out, "c_sum": c_sum, "c_apply": c_apply,
                "q": lambda t, k: qk(t, 0, k), "k": lambda t, k: qk(t, 1, k), "v": v, "scores": scores, "weights": weights, "attend": attend,
            }
            PER_ITERATION = 64

            def body(t, todo):
                if not isinstance(t, int):
                    links[0] = links[0] + links[1] + (t - 3) * PER_ITERATION
                    links[1] = 0
                run(steps, todo, t)
                if not isinstance(t, int):
                    assert links[1] == PER_ITERATION, links[1]
                    links[0], links[1] = base[0] + (NB - 3) * PER_ITERATION, 0
                else:
                    links[0], links[1] = links[0] + links[1], 0
                    base[0] = links[0]

            base = [0]
            pipeline(dve, body)

        @block.gpsimd
        def _(pool):
            gp = nc.gpsimd
            gp.memset(bias_rows[:, :, :].bitcast(F32), 0.0).then_inc(s_pool_c, 1)
            for l in range(LAYERS):
                gp.memset(pick_bias[l][:, :].bitcast(F32), 0.0).then_inc(s_pool_c, 1)
            gp.memset(ident[:, :], 1.0).then_inc(s_pool_c, 1)
            gp.memset(mask_up[:, :], 1.0).then_inc(s_pool_c, 1)
            pool.wait_ge(s_pool_c, 5)
            gp.affine_select(out=ident[:, :], in_=ident[:, :], pattern=[[-1, P]], compare_op=ALU.is_equal, fill=0.0,
                             base=0, channel_multiplier=1).then_inc(s_pool_c, 1)
            gp.affine_select(out=mask_low[:, :], in_=mask_up[:, :], pattern=[[1, P]], compare_op=ALU.is_gt, fill=0.0,
                             base=0, channel_multiplier=-1).then_inc(s_pool_c, 1)
            pool.wait_ge(s_pool_c, 7)
            gp.affine_select(out=mask_up[:, :], in_=mask_up[:, :], pattern=[[-1, P]], compare_op=ALU.is_gt, fill=0.0,
                             base=0, channel_multiplier=1).then_inc(s_pool_c, 1)
            pool.wait_ge(s_pool_c, 8)
            pool.wait_ge(s_setup, 1)

            def graph_turn(n):
                pool.wait_ge(s_at_lo, n + 1)
                wait(pool, s_mix, 2 * n)
                for part in range(2):
                    blocks = attT[part][:, :, :].rearrange("p j (i q) -> p (j i) q", i=NT)[:, 0::3, :]
                    for dst, keep in ((up, mask_up), (low, mask_low)):
                        ins = gp.tensor_tensor(dst[part][:, :, :], blocks,
                                               keep[:, :].unsqueeze(1).to_broadcast([P, NT, P]), ALU.mult)
                ins.then_inc(s_cut, 1)

            def q(t, g):
                s = t - 2
                if g == 0:
                    pool.wait_ge(s_adj["c"], 16 * (s + 1))
                    wait(pool, s_msk, NT * NH * s)
                    wait(pool, s_v_all, NT * s)
                    apart(pool)
                    gp.tensor_scalar(neg_adj[:, :, :], adj_in[:, :, :], 0.0, MASKED / SCALE, ALU.is_le, ALU.mult
                                     ).then_inc(s_pool, 1)
                    gp.tensor_scalar(bias_adj[:, :, :], adj_in[:, :, :], 0.0, beta_col[:, 0:1], ALU.max, ALU.mult
                                     ).then_inc(s_pool, 1)
                    pool.wait_ge(s_pool, 2 * (s + 1))
                    gp.tensor_tensor(bias_adj[:, :, :], bias_adj[:, :, :], neg_adj[:, :, :], ALU.add).then_inc(s_badj, 1)
                if g == 2:
                    pool.wait_ge(s_y, NT * (s + 1))
                    wait(pool, s_out_ok, NT * s)
                    gp.tensor_tensor(res[:, :, :], y_in[:, :, :], v_bias[:, :].unsqueeze(1).to_broadcast([P, NT, D]),
                                     ALU.add).then_inc(s_res, 1)

            def v(t, i):
                s = t - 2
                pool.wait_ge(s_v_rd, NT * s + i + 1)
                wait(pool, s_pv, NH * s)
                apart(pool)
                rest = v_rest[:, i, :].rearrange("p (h d) -> p h d", h=NH)
                gp.tensor_copy(v_parts[:, i, :, 1, :], rest).then_inc(s_v_mid, 1)
                pool.wait_ge(s_v_mid, NT * s + i + 1)
                gp.tensor_tensor(v_parts[:, i, :, 2, :], rest, v_parts[:, i, :, 1, :], ALU.subtract).then_inc(s_v_all, 1)

            steps = {
                "a_turn": lambda t, k: graph_turn(layer_a(t)), "b_turn": lambda t, k: graph_turn(layer_b(t)),
                "q": q, "v": v,
            }
            pipeline(pool, lambda t, todo: run(steps, todo, t))


_WEIGHTS_T = ("L0_gnn_Wl", "L0_gnn_Ws", "L0_gnn_Wr")
_INS = ["x", "adj", "L0_gnn_Wl", "L0_gnn_Ws", "L0_gnn_Wr", "L0_gnn_bl", "L0_gnn_bs", "L0_gnn_br",
        "L0_gnn_ln_w", "L0_gnn_ln_b", "L1_gnn_Wq", "L1_gnn_Wk", "L1_gnn_Wv", "L1_gnn_bq", "L1_gnn_bk",
        "L1_gnn_bv", "L1_gnn_beta"]


def kernel(**inputs):
    import concourse.bacc as _bacc
    from concourse.bass_utils import run_bass_kernel_spmd as _run

    nc = _bacc.Bacc("TRN2", target_bir_lowering=False, num_devices=1)
    arrays, args = {}, []
    for name in _INS:
        a = np.asarray(inputs[name])
        if name in _WEIGHTS_T:
            a = a.transpose(0, 2, 1)
        if a.ndim == 0:
            a = a.reshape(1)
        a = np.ascontiguousarray(a)
        arrays[f"in_{name}"] = a
        args.append(nc.dram_tensor(f"in_{name}", a.shape, mybir.dt.from_np(a.dtype), kind="ExternalInput").ap())
    shape = arrays["in_x"].shape
    args.append(nc.dram_tensor("out_0", shape, F32, kind="ExternalOutput").ap())
    graph_attention_kernel(nc, *args)
    r = _run(nc, [arrays], core_ids=[0])
    return r.results[0]["out_0"]
```

```python
from contextlib import ExitStack

import numpy as np

import concourse.bass as bass
from concourse import mybir

F32 = mybir.dt.float32
F32R = mybir.dt.float32r
BF16 = mybir.dt.bfloat16
F16 = mybir.dt.float16
ALU = mybir.AluOpType
ACT = mybir.ActivationFunctionType
AX = mybir.AxisListType

P = 128
NH = 12
VP = 3
SLOTS = 3
EPS_GRAPH = 1e-12
EPS_NORM = 1e-5
EPS_ATTN = 1e-10
MASKED = -9000000000000000.0
BIG = 3.0e38
PARTS = ((0, 0), (0, 1), (1, 0))


ORDER = {
    "pe": """
        late_weights.10 late_attend.9 late_weights.11 q.0 late_attend.10 late_attend.11 q.1 q.2 k.0 turn_h.0 k.1
        turn_h.1 k.2 v.0 turn_h.2 v.1 b_scores.0 b_proj.0 turn_x.0 b_proj.1 b_proj.2 b_turn.0 b_proj.3 b_proj.4
        scores.0 turn_x.1 turn_x.2 scores.1 weights.0 b_proj.5 scores.2 a_scores.0 b_mix.0 weights.1 scores.3
        attend.0 b_mix.1 scores.4 attend.1 weights.2 a_proj.0 scores.5 weights.3 a_proj.1 attend.2 scores.6
        a_proj.2 attend.3 a_turn.0 weights.4 scores.7 a_proj.3 weights.5 attend.4 scores.8 weights.6 attend.5
        a_proj.4 weights.7 attend.6 scores.9 a_proj.5 weights.8 turn_y.0 scores.10 attend.7 a_mix.0 weights.9
        attend.8 scores.11 turn_y.1 a_mix.1 turn_y.2""",
    "act": """
        late_weights.10 late_weights.11 q.0 q.1 h_norm.0 q.2 k.0 turn_h.0 k.1 turn_h.1 k.2 v.0 turn_h.2 v.1
        b_proj.0 turn_x.0 b_proj.1 b_scores.0 b_turn.0 b_proj.2 c_norm.0 b_proj.3 turn_x.1 scores.0 b_proj.4
        c_store.0 turn_x.2 weights.0 b_proj.5 scores.1 scores.2 a_scores.0 weights.1 scores.3 weights.2 scores.4
        a_proj.0 b_norm.0 a_proj.1 weights.3 scores.5 b_apply.0 a_turn.0 weights.4 scores.6 weights.5 scores.7
        a_proj.2 weights.6 scores.8 a_proj.3 weights.7 a_proj.4 b_norm2.0 scores.9 a_proj.5 weights.8 turn_y.0
        scores.10 weights.9 turn_y.1 scores.11 turn_y.2""",
    "dve": """
        late_weights.10 late_attend.9 late_weights.11 late_attend.10 late_attend.11 h_norm.0 c_sum.0 q.0 q.1
        h_apply.0 q.2 turn_h.0 k.0 c_stat.0 k.1 k.2 turn_h.1 v.0 turn_h.2 v.1 b_proj.0 b_scores.0 b_proj.1
        b_mask.0 c_stat.1 turn_x.0 c_norm.0 b_turn.0 b_proj.2 c_apply.0 scores.0 b_proj.3 turn_x.1 scores.1
        b_proj.4 turn_x.2 b_proj.5 weights.0 scores.2 a_scores.0 b_mix.0 scores.3 attend.0 weights.1 b_mix.1
        scores.4 weights.2 b_norm.0 attend.1 a_proj.0 b_apply.0 attend.2 scores.5 a_mask.0 weights.3 scores.6
        a_proj.1 attend.3 weights.4 a_turn.0 scores.7 weights.5 b_resid.0 attend.4 scores.8 a_proj.2 weights.6
        attend.5 attend.6 a_proj.3 b_resid.1 b_norm2.0 weights.7 scores.9 b_out.0 a_proj.4 a_proj.5 weights.8
        turn_y.0 scores.10 attend.7 a_mix.0 attend.8 weights.9 scores.11 turn_y.1 a_mix.1 turn_y.2""",
    "pool": """
        q.0 c_sum.0 q.2 v.0 b_turn.0 v.1 b_apply.0 a_turn.0""",
}

STAGE_D = ("late_weights", "late_attend", "c_sum", "c_stat", "c_norm", "c_apply", "c_store")
STAGE_C = ("q", "k", "v", "scores", "weights", "attend")


def schedule(engine, a, b, c, d):
    steps = []
    for word in ORDER[engine].split():
        name, k = word.split(".")
        if name in STAGE_D:
            on = d
        elif name in STAGE_C:
            on = c
        else:
            on = a if name.startswith("a_") or name == "turn_x" else b
        if on:
            steps.append((name, int(k)))
    return steps


def graph_attention_kernel(nc, x, adj, wl, ws, wr, bl, bs, br, ln_w, ln_b,
                           wq, wk, wv, bq, bk, bv, beta, out):
    NB, S, D = x.shape
    NT = S // P
    NC = D // P
    HD = D // NH
    HPG = P // HD
    LAYERS = wl.shape[0]
    TEMPER = float(D) ** -0.5
    SCALE = float(HD) ** -0.5
    assert NT == 2 and NC == 3 and LAYERS == 2 and HD == 32

    x_v = x.rearrange("b (i p) d -> b p i d", p=P)
    adj_v = adj.rearrange("b (i p) j -> b p i j", p=P)
    out_v = out.rearrange("b (i p) d -> b p i d", p=P)

    with ExitStack() as ctx:
        def sb(name, shape, dt=F32):
            return ctx.enter_context(nc.sbuf_tensor(name, shape, dt))

        def bank(name):
            return ctx.enter_context(nc.psum_tensor(name, [P, 512], F32))

        def sem(name):
            return ctx.enter_context(nc.semaphore(name))

        w_graph = [[sb(f"w_graph{l}{p}", [P, NC, 3, D], F32R) for p in "hl"] for l in range(LAYERS)]
        w_qkv = [sb(f"w_qkv{p}", [P, NC, 3, D], F32R) for p in "hl"]
        bias_rows = sb("bias_rows", [P, 3, D], F32R)
        pick_bias = [sb(f"pick_bias{l}", [P, P], F32R) for l in range(LAYERS)]
        ident = sb("ident", [P, P])
        mask_up = sb("mask_up", [P, P])
        mask_low = sb("mask_low", [P, P])
        q_bias = sb("q_bias", [P, NC])
        k_bias = sb("k_bias", [P, NC])
        v_bias = sb("v_bias", [P, D])
        g1_col = sb("g1_col", [P, NC])
        b1_col = sb("b1_col", [P, NC])
        g2_row = sb("g2_row", [P, D])
        b2_row = sb("b2_row", [P, D])
        beta_col = sb("beta_col", [P, 1])
        x_in = sb("x_in", [P, NT, D])
        adj_in = sb("adj_in", [P, NT, S])
        hT_ac = [sb(f"hT_ac{p}", [P, NC, S], F32R) for p in "hl"]
        hT_b = [sb(f"hT_b{p}", [P, NC, S], F32R) for p in "hl"]
        expu = sb("expu", [P, NT, S])
        attT = [sb(f"attT{p}", [P, NT, S], F32R) for p in "hl"]
        up = [sb(f"up{p}", [P, NT, P], F32R) for p in "hl"]
        low = [sb(f"low{p}", [P, NT, P], F32R) for p in "hl"]
        hlr = [sb(f"hlr{p}", [P, NT, 2, D], F32R) for p in "hl"]
        self_part = sb("self_part", [P, NT, D])
        mixed = sb("mixed", [P, NT, D])
        normed = sb("normed", [P, NT, D])
        diag_tmp = sb("diag_tmp", [P, NT, P], BF16)
        y_in = sb("y_in", [P, NT, D])
        res = sb("res", [P, NT, D])
        bias_adj = sb("bias_adj", [P, NT, S])
        qk_hi = sb("qk_hi", [P, 2, NC, S], F32R)
        qk_lo = sb("qk_lo", [P, 2, NC, S], F32R)
        q_st = sb("q_st", [P, NH, S], F32R)
        k_st = sb("k_st", [P, NH, S], F32R)
        v_parts = sb("v_parts", [P, NT, NH, VP, HD], BF16)
        v_rest = sb("v_rest", [P, NT, D])
        neg_adj = v_rest[:, :, 0:S]
        masked = sb("masked", [P, NT, S])
        prob = sb("prob", [P, 2, NT, S])
        pT_hi = sb("pT_hi", [P, 2, NT, S], F16)
        pT_lo = sb("pT_lo", [P, 2, NT, S], F16)
        result = sb("result", [P, NT, D])
        att = result[:, :, :].rearrange("p i (h d) -> p i h d", h=NH)
        negmax = sb("negmax", [P, NT])
        ubias = sb("ubias", [P, NT])
        zsum = sb("zsum", [P, NT])
        ssum = sb("ssum", [P, NT])
        diag = sb("diag", [P, NT])
        inv_s = {k: sb(f"inv_s_{k}", [P, NT]) for k in "ab"}
        hmin = sb("hmin", [P, NT, NH])
        hsum = sb("hsum", [P, NT, NH])
        hinv = sb("hinv", [P, NT, NH])
        norms = ("a", "b", "y", "c")
        stats = {k: sb(f"stats_{k}", [P, NT, 6]) for k in norms}
        mv = {k: sb(f"mv_{k}", [P, NT, 2]) for k in norms}
        var = {k: sb(f"var_{k}", [P, NT]) for k in "ab"}
        var.update({k: mv[k][:, :, 1] for k in "yc"})
        eps = {"a": EPS_GRAPH, "b": EPS_GRAPH, "y": EPS_NORM, "c": EPS_NORM}
        shift = sb("shift", [P, NT])
        inv_s2 = {k: sb(f"inv_s2_{k}", [P, NT]) for k in "ab"}
        eps_col = {EPS_GRAPH: sb("eps_graph", [P, 1]), EPS_NORM: sb("eps_norm", [P, 1])}
        lnv = {k: sb(f"lnv_{k}", [P, NT]) for k in norms}
        y0 = {k: sb(f"y0_{k}", [P, NT]) for k in norms}
        tmp = {k: sb(f"tmp_{k}", [P, NT]) for k in norms}
        rstd = {k: sb(f"rstd_{k}", [P, NT]) for k in norms}

        def flat(ap):
            return ap.rearrange("p i j -> p (i j)")[:, 0:D]

        staging = [flat(prob[:, 0, :, :]), flat(prob[:, 1, :, :]), flat(bias_adj[:, :, :])]
        staging += [y_in[:, i, :] for i in range(NT)] + [flat(masked[:, :, :])]
        staging += [buf[:, i, :] for buf in (res, result, v_rest) for i in range(NT)]
        BATCH = 3 * NC

        bank_w = [bank("bank_w0"), bank("bank_w1")]
        bank_u = bank("bank_u")
        bank_t = bank("bank_t")
        bank_m = bank("bank_m")
        bank_s = bank("bank_s")
        bank_p = bank("bank_p")
        bank_o = bank("bank_o")

        s_setup = sem("s_setup")
        s_const = sem("s_const")
        s_stage = [sem(f"s_stage{n}") for n in range(3)]
        s_w_hi, s_split = sem("s_w_hi"), sem("s_split")
        s_pool_c = sem("s_pool_c")
        s_xa, s_xb = sem("s_xa"), sem("s_xb")
        s_adj = {k: sem(f"s_adj_{k}") for k in "abc"}
        s_tx_pe, s_tx_hi, s_tx_lo = sem("s_tx_pe"), sem("s_tx_hi"), sem("s_tx_lo")
        s_th_pe, s_th_f, s_th_lo = sem("s_th_pe"), sem("s_th_f"), sem("s_th_lo")
        s_ty_pe, s_ty_hi, s_ty_lo = sem("s_ty_pe"), sem("s_ty_hi"), sem("s_ty_lo")
        s_u, s_ub, s_exp, s_em = sem("s_u"), sem("s_ub"), sem("s_exp"), sem("s_em")
        s_proj, s_proj_hi, s_proj_rd = sem("s_proj"), sem("s_proj_hi"), sem("s_proj_rd")
        s_at, s_at_hi, s_at_lo, s_cut = sem("s_at"), sem("s_at_hi"), sem("s_at_lo"), sem("s_cut")
        s_mix, s_mix_rd = sem("s_mix"), sem("s_mix_rd")
        s_var = {k: sem(f"s_var_{k}") for k in norms}
        s_ln = {k: sem(f"s_ln_{k}") for k in norms}
        s_y0 = {k: sem(f"s_y0_{k}") for k in norms}
        s_self, s_diag = sem("s_self"), sem("s_diag")
        s_shift, s_scaled, s_affine, s_affine_mid = sem("s_shift"), sem("s_scaled"), sem("s_affine"), sem("s_affine_mid")
        s_hinv, s_csum, s_csum_mid = sem("s_hinv"), sem("s_csum"), sem("s_csum_mid")
        s_h1, s_resid, s_y = sem("s_h1"), sem("s_resid"), sem("s_y")
        s_res, s_badj = sem("s_res"), sem("s_badj")
        s_qk, s_qk_hi, s_qk_lo = sem("s_qk"), sem("s_qk_hi"), sem("s_qk_lo")
        s_stack = {k: sem(f"s_stack_{k}") for k in "qk"}
        s_v, s_v_hi, s_v_rd, s_v_all, s_v_mid = sem("s_v"), sem("s_v_hi"), sem("s_v_rd"), sem("s_v_all"), sem("s_v_mid")
        s_sc, s_msk, s_prob = sem("s_sc"), sem("s_msk"), sem("s_prob")
        s_pt, s_pt_hi, s_pt_lo = sem("s_pt"), sem("s_pt_hi"), sem("s_pt_lo")
        s_pv, s_att = sem("s_pv"), sem("s_att")
        s_out_ok, s_out = sem("s_out_ok"), sem("s_out")
        s_apart = sem("s_apart")
        s_dve, s_pool = sem("s_dve"), sem("s_pool")

        def wait(eng, s, count):
            if not (isinstance(count, int) and count <= 0):
                eng.wait_ge(s, count)

        def apart(eng):
            eng.sem_inc(s_apart, 1)

        STACKED = 16 * SLOTS * HPG

        def layer_a(t):
            return 2 * t

        def layer_b(t):
            return 2 * t - 1

        def run(steps, todo, t):
            for name, k in todo:
                if name in steps:
                    steps[name](t, k)

        def pipeline(eng, order, body):
            def with_split(before, n, todo):
                at = todo.index(before) if before in todo else 0
                return todo[:at] + [("split", n)] + todo[at:]

            body(0, with_split(("a_proj", 0), 0, schedule(order, True, False, False, False)))
            body(1, with_split(("b_proj", 0), 1, schedule(order, True, True, False, False)))
            body(2, with_split(("q", 0), 2, schedule(order, True, True, True, False)))
            with eng.Fori(3, NB) as t:
                body(t, schedule(order, True, True, True, True))
            body(NB, schedule(order, False, True, True, True))
            body(NB + 1, schedule(order, False, False, True, True))
            body(NB + 2, schedule(order, False, False, False, True))

        block = ctx.enter_context(nc.Block())

        @block.sync
        def _(sp):
            def stack(c, which):
                side = "qk".index(which)
                wait(sp, s_qk_lo, NC * (2 * c + side + 1))
                apart(sp)
                for slot in range(SLOTS):
                    part = (qk_hi, (qk_lo, qk_hi)[side], (qk_hi, qk_lo)[side])[slot]
                    for r in range(HPG):
                        sp.dma_start((q_st, k_st)[side][slot * HD:(slot + 1) * HD, r::HPG, :].bitcast(F32),
                                     part[r * HD:(r + 1) * HD, side, :, :].bitcast(F32)).then_inc(s_stack[which], 16)

            def body(t, todo):
                names = [n for n, _ in todo]
                in_a, in_b, in_c = "a_scores" in names, "b_scores" in names, "scores" in names
                if in_c:
                    wait(sp, s_em, 2 * (layer_a(t - 1) + 1) if not (isinstance(t, int) and t > NB)
                         else 2 * (layer_b(t - 1) + 1))
                    apart(sp)
                    sp.dma_start(adj_in[:, :, :], adj_v[t - 2]).then_inc(s_adj["c"], 16)
                if in_a:
                    wait(sp, s_resid, (t - 1) * NT)
                    if isinstance(t, int) and t == 1:
                        sp.wait_ge(s_tx_pe, NC)
                    apart(sp)
                    sp.dma_start(x_in[:, :, :], x_v[t]).then_inc(s_xa, 16)
                if in_c:
                    stack(t - 2, "q")
                if in_b:
                    if in_c:
                        wait(sp, s_badj, t - 1)
                    else:
                        wait(sp, s_em, 2 * (layer_a(t - 1) + 1))
                    apart(sp)
                    sp.dma_start(adj_in[:, :, :], adj_v[t - 1]).then_inc(s_adj["b"], 16)
                if in_c:
                    stack(t - 2, "k")
                if in_b:
                    if in_a:
                        wait(sp, s_tx_pe, NC * (t + 1))
                    else:
                        wait(sp, s_resid, (t - 1) * NT)
                    apart(sp)
                    sp.dma_start(x_in[:, :, :], x_v[t - 1]).then_inc(s_xb, 16)
                if in_a:
                    if in_b:
                        wait(sp, s_em, 2 * (layer_b(t) + 1))
                    apart(sp)
                    sp.dma_start(adj_in[:, :, :], adj_v[t]).then_inc(s_adj["a"], 16)

            def load(n):
                mats = [w[n] for w in (wl, ws, wr)] if n < LAYERS else (wq, wk, wv)
                for k in range(BATCH):
                    q = BATCH * n + k
                    wait(sp, s_split, q - len(staging) + 1)
                    sp.dma_start(staging[q % len(staging)], mats[k // NC][k % NC * P:(k % NC + 1) * P, :]
                                 ).then_inc(s_stage[n], 16)

            def body_and_weights(t, todo):
                body(t, todo)
                for n in {0: (0, 1), 1: (2,)}.get(t, ()) if isinstance(t, int) else ():
                    load(n)

            pipeline(sp, "pe", body_and_weights)
            sp.wait_ge(s_out, 16 * NB)

        @block.tensor
        def _(pe):
            def mm(dst, lhsT, rhs, start, stop):
                return nc.tensor.matmul(dst, lhsT, rhs, start=start, stop=stop)

            def turn_x(t, k):
                pe.wait_ge(s_xa, 16 * (t + 1))
                wait(pe, s_th_lo, NC * t) if k == 0 else None
                wait(pe, s_tx_lo, NC * t + k)
                for i in range(NT):
                    last = nc.tensor.transpose(bank_t[:, i * P:(i + 1) * P], x_in[:, i, k * P:(k + 1) * P], ident[:, :])
                last.then_inc(s_tx_pe, 1)

            def turn_h(t, k):
                pe.wait_ge(s_h1, NT * t)
                if k == 0:
                    wait(pe, s_ty_lo, NC * (t - 1))
                    pe.wait_ge(s_tx_lo, NC * t)
                wait(pe, s_th_lo, NC * (t - 1) + k)
                for i in range(NT):
                    last = nc.tensor.transpose(bank_t[:, i * P:(i + 1) * P], normed[:, i, k * P:(k + 1) * P], ident[:, :])
                last.then_inc(s_th_pe, 1)

            def turn_y(t, k):
                pe.wait_ge(s_y, NT * t)
                if k == 0:
                    pe.wait_ge(s_th_lo, NC * t)
                    if not (isinstance(t, int) and t == NB):
                        pe.wait_ge(s_tx_lo, NC * (t + 1))
                wait(pe, s_ty_lo, NC * (t - 1) + k)
                for i in range(NT):
                    last = nc.tensor.transpose(bank_t[:, i * P:(i + 1) * P], y_in[:, i, k * P:(k + 1) * P], ident[:, :])
                last.then_inc(s_ty_pe, 1)

            def graph_scores(n, hT, ready):
                ready()
                wait(pe, s_at_lo, n)
                for i in range(NT):
                    for c in range(NC):
                        for a, b in PARTS:
                            last = mm(bank_u[:, i * S:(i + 1) * S], hT[a][:, c, i * P:(i + 1) * P], hT[b][:, c, :],
                                      c == 0 and (a, b) == PARTS[0], c == NC - 1 and (a, b) == PARTS[-1])
                last.then_inc(s_u, 1)

            def a_scores(t, _k):
                graph_scores(layer_a(t), hT_ac, lambda: pe.wait_ge(s_tx_lo, NC * (t + 1)))

            def b_scores(t, _k):
                graph_scores(layer_b(t), hT_b, lambda: pe.wait_ge(s_th_lo, NC * t))

            def projection(n, layer, hT, j):
                m, i = j // 2, j % 2
                if j in (2, 3):
                    pe.wait_ge(s_proj_rd, 4 * n + j - 1)
                if j >= 4:
                    pe.wait_ge(s_self, 2 * n + j - 3)
                for c in range(NC):
                    for a, b in PARTS:
                        mm(bank_w[i][:, 0:D], hT[a][:, c, i * P:(i + 1) * P], w_graph[layer][b][:, c, m, :],
                           c == 0 and (a, b) == PARTS[0], False)
                mm(bank_w[i][:, 0:D], pick_bias[layer][:, :], bias_rows[:, m, :], False, True).then_inc(s_proj, 1)

            def a_proj(t, j):
                if j < 2:
                    wait(pe, s_proj_rd, 4 * layer_a(t) - 1 + j)
                if j == 0:
                    pe.wait_ge(s_tx_lo, NC * (t + 1))
                projection(layer_a(t), 0, hT_ac, j)

            def b_proj(t, j):
                if j < 2:
                    wait(pe, s_proj_rd, 4 * layer_b(t) - 1 + j)
                    wait(pe, s_v_rd, NT * (t - 1) - 1 + j)
                if j == 0:
                    pe.wait_ge(s_th_lo, NC * t)
                projection(layer_b(t), 1, hT_b, j)

            def graph_turn(n):
                pe.wait_ge(s_em, 2 * (n + 1))
                for j in range(NT):
                    for i in range(NT):
                        last = nc.tensor.transpose(bank_u[:, j * S + i * P:j * S + (i + 1) * P],
                                                   expu[:, i, j * P:(j + 1) * P], ident[:, :])
                last.then_inc(s_at, 1)

            def mix(n, i):
                pe.wait_ge(s_cut, n + 1)
                pe.wait_ge(s_proj_rd, 4 * (n + 1))
                wait(pe, s_mix_rd, 2 * n + i)
                other = 1 - i
                terms = ((up, i, None, i, 0), (low, i, None, i, 1), (attT, other, i, other, i))
                count = 0
                for src, jb, ib, j, side in terms:
                    for a, b in PARTS:
                        w = src[a][:, jb, :] if ib is None else src[a][:, jb, ib * P:(ib + 1) * P]
                        last = mm(bank_m[:, 0:D], w, hlr[b][:, j, side, :], count == 0, count == 8)
                        count += 1
                last.then_inc(s_mix, 1)

            def qk(t, side, g):
                s, j = t - 2, NC * side + g
                if j == 0:
                    pe.wait_ge(s_ty_lo, NC * (t - 1))
                if j < 2:
                    last_layer = layer_b(t - 1) if isinstance(t, int) and t == NB + 1 else layer_a(t - 1)
                    pe.wait_ge(s_proj_rd, 4 * last_layer + 3 + j)
                else:
                    pe.wait_ge(s_qk_lo, 6 * s + j - 1)
                for c in range(NC):
                    for a, b in PARTS:
                        last = mm(bank_w[j % 2][:, 0:S], w_qkv[a][:, c, side, g * P:(g + 1) * P], hT_ac[b][:, c, :],
                                  c == 0 and (a, b) == PARTS[0], c == NC - 1 and (a, b) == PARTS[-1])
                last.then_inc(s_qk, 1)

            def v(t, i):
                s = t - 2
                pe.wait_ge(s_qk_lo, 6 * s + 5 + i)
                for c in range(NC):
                    for a, b in PARTS:
                        last = mm(bank_w[i][:, 0:D], hT_ac[a][:, c, i * P:(i + 1) * P], w_qkv[b][:, c, 2, :],
                                  c == 0 and (a, b) == PARTS[0], c == NC - 1 and (a, b) == PARTS[-1])
                last.then_inc(s_v, 1)

            def scores(t, h):
                s = t - 2
                if h == 0:
                    pe.wait_ge(s_stack["q"], STACKED * (s + 1))
                    pe.wait_ge(s_stack["k"], STACKED * (s + 1))
                wait(pe, s_msk, NT * (NH * s + h))
                for i in range(NT):
                    last = mm(bank_s[:, i * S:(i + 1) * S], q_st[0:SLOTS * HD, h, i * P:(i + 1) * P],
                              k_st[0:SLOTS * HD, h, :], True, True)
                last.then_inc(s_sc, 1)

            def weights(t, h):
                s = t - 2
                pe.wait_ge(s_prob, NT * (NH * s + h + 1))
                wait(pe, s_pt_lo, NH * s + h)
                for j in range(NT):
                    for i in range(NT):
                        last = nc.tensor.transpose(bank_p[:, j * S + i * P:j * S + (i + 1) * P],
                                                   prob[:, h % 2, i, j * P:(j + 1) * P], ident[:, :])
                last.then_inc(s_pt, 1)

            def attend(t, h):
                s = t - 2
                pe.wait_ge(s_pt_lo, NH * s + h + 1)
                if h == 0:
                    pe.wait_ge(s_v_all, NT * (s + 1))
                if h % 2 == 0:
                    wait(pe, s_att, NH // 2 * s + h // 2)
                for i in range(NT):
                    at = (2 * i + h % 2) * VP * HD
                    for j in range(NT):
                        vp = v_parts[:, j, h, :, :].rearrange("p a d -> p (a d)")
                        mm(bank_o[:, at:at + VP * HD], pT_hi[:, h % 2, j, i * P:(i + 1) * P], vp, j == 0, False)
                        last = mm(bank_o[:, at:at + 2 * HD], pT_lo[:, h % 2, j, i * P:(i + 1) * P], vp[:, 0:2 * HD],
                                  False, j == NT - 1)
                last.then_inc(s_pv, 1)

            steps = {
                "split": lambda t, n: pe.wait_ge(s_setup, n + 1),
                "turn_x": turn_x, "turn_h": turn_h, "turn_y": turn_y,
                "a_scores": a_scores, "b_scores": b_scores, "a_proj": a_proj, "b_proj": b_proj,
                "a_turn": lambda t, k: graph_turn(layer_a(t)), "b_turn": lambda t, k: graph_turn(layer_b(t)),
                "a_mix": lambda t, k: mix(layer_a(t), k), "b_mix": lambda t, k: mix(layer_b(t), k),
                "q": lambda t, k: qk(t, 0, k), "k": lambda t, k: qk(t, 1, k), "v": v, "scores": scores, "weights": weights, "late_weights": lambda t, k: weights(t - 1, k), "attend": attend,
                "late_attend": lambda t, k: attend(t - 1, k),
            }
            pe.wait_ge(s_pool_c, 6)
            pipeline(pe, "pe", lambda t, todo: run(steps, todo, t))

        @block.scalar
        def _(act):
            nc.scalar.preload_act_table_set("natural_log_exp_and_others")

            for m, b in enumerate((bl, bs, br)):
                for half in range(2):
                    act.dma_start((self_part, self_part, mixed)[m][32 * half:32 * half + LAYERS, m % 2, :], b
                                  ).then_inc(s_const, 16)
            for col, v in ((q_bias, bq), (k_bias, bk), (g1_col, ln_w[0, :]), (b1_col, ln_b[0, :])):
                act.dma_start(col[:, :], v.rearrange("(g p) -> p g", p=P), allow_slow_non_contiguous=True
                              ).then_inc(s_const, 16)
            for row, v in ((v_bias, bv), (g2_row, ln_w[1, :]), (b2_row, ln_b[1, :]), (beta_col, beta)):
                act.dma_start(row[:, :], v.partition_broadcast(P)).then_inc(s_const, 16)

            def split(_t, n):
                act.wait_ge(s_stage[n], 16 * BATCH)
                w = (w_graph[0], w_graph[1], w_qkv)[n]
                for k in range(BATCH):
                    nc.scalar.activation(w[0][:, k % NC, k // NC, :], staging[(BATCH * n + k) % len(staging)], ACT.Copy
                                         ).then_inc(s_w_hi, 1)

            def turn_x(t, k):
                act.wait_ge(s_tx_pe, NC * t + k + 1)
                if k == 0:
                    wait(act, s_v, NT * (t - 1))
                nc.scalar.activation(hT_ac[0][:, k, :], bank_t[:, 0:S], ACT.Copy).then_inc(s_tx_hi, 1)

            def turn_y(t, k):
                act.wait_ge(s_ty_pe, NC * (t - 1) + k + 1)
                if k == 0 and not (isinstance(t, int) and t == NB):
                    act.wait_ge(s_proj, 6 * layer_a(t) + 6)
                nc.scalar.activation(hT_ac[0][:, k, :], bank_t[:, 0:S], ACT.Copy).then_inc(s_ty_hi, 1)

            def turn_h(t, k):
                act.wait_ge(s_th_pe, NC * (t - 1) + k + 1)
                f = mixed[:, 0, 0:S] if k == 0 else (mixed[:, 1, 0:S] if k == 1 else self_part[:, 0, 0:S])
                for dst in (f, hT_b[0][:, k, :]):
                    nc.scalar.activation(dst, bank_t[:, 0:S], ACT.Relu, bias=b1_col[:, k:k + 1],
                                         scale=g1_col[:, k:k + 1]).then_inc(s_th_f, 1)

            def graph_exp(n):
                act.wait_ge(s_ub, n + 1)
                wait(act, s_at, n)
                for i in range(NT):
                    nc.scalar.activation(expu[:, i, :], bank_u[:, i * S:(i + 1) * S], ACT.Exp, bias=ubias[:, i:i + 1],
                                         scale=TEMPER, accum_out=zsum[:, i:i + 1]).then_inc(s_exp, 1)

            def proj_hi(n, j):
                m, i = j // 2, j % 2
                act.wait_ge(s_proj, 6 * n + j + 1)
                if m == 1:
                    act.wait_ge(s_diag, NT * (n + 1))
                    wait(act, s_mix_rd, 2 * n)
                    nc.scalar.activation(self_part[:, i, :], bank_w[i][:, 0:D], ACT.Copy,
                                         scale=diag[:, i:i + 1]).then_inc(s_self, 1)
                else:
                    if j == 0:
                        wait(act, s_mix, 2 * n)
                    nc.scalar.activation(hlr[0][:, i, m // 2, :], bank_w[i][:, 0:D], ACT.Copy).then_inc(s_proj_hi, 1)

            def graph_turn(n):
                act.wait_ge(s_at, n + 1)
                wait(act, s_mix, 2 * n)
                wait(act, s_cut, n)
                nc.scalar.activation(attT[0][:, :, :].rearrange("p j i -> p (j i)"), bank_u[:, :], ACT.Copy).then_inc(s_at_hi, 1)

            def root(k, index):
                act.wait_ge(s_var[k], (index + 1) * (NT if k in "yc" else 1))
                nc.scalar.activation(lnv[k][:, :], var[k] if k in "yc" else var[k][:, :], ACT.Ln,
                                     bias=eps_col[eps[k]][:, :]).then_inc(s_ln[k], 1)
                act.wait_ge(s_ln[k], index + 1)
                nc.scalar.activation(y0[k][:, :], lnv[k][:, :], ACT.Exp, scale=-0.5).then_inc(s_y0[k], 1)

            def b_apply(t, _k):
                act.wait_ge(s_shift, t)
                for i in range(NT):
                    nc.scalar.activation(normed[:, i, :], mixed[:, i, :], ACT.Identity, bias=shift[:, i:i + 1],
                                         scale=rstd["b"][:, i:i + 1]).then_inc(s_scaled, 1)

            def c_norm(t, _k):
                root("c", t - 3)

            def c_store(t, _k):
                act.wait_ge(s_out_ok, (t - 2) * NT)
                act.dma_start(out_v[t - 3], result[:, :, :]).then_inc(s_out, 16)

            def qk(t, side, g):
                s, j = t - 2, NC * side + g
                act.wait_ge(s_qk, 6 * s + j + 1)
                wait(act, s_stack["qk"[side]], STACKED * s)
                nc.scalar.activation(qk_hi[:, side, g, :], bank_w[j % 2][:, 0:S], ACT.Identity,
                                     bias=(q_bias, k_bias)[side][:, g:g + 1]).then_inc(s_qk_hi, 1)

            def v(t, i):
                s = t - 2
                act.wait_ge(s_v, NT * s + i + 1)
                if i == 0:
                    wait(act, s_pv, NH * s)
                nc.scalar.activation(v_parts[:, i, :, 0, :], bank_w[i][:, 0:D].rearrange("p (h d) -> p h d", h=NH),
                                     ACT.Copy).then_inc(s_v_hi, 1)

            def scores(t, h):
                s = t - 2
                wait(act, s_pt, NH * s + max(h - 1, 0))
                for i in range(NT):
                    act.wait_ge(s_msk, NT * (NH * s + h) + i + 1)
                    nc.scalar.activation(prob[:, h % 2, i, :], masked[:, i, :], ACT.Exp, bias=hmin[:, i, h:h + 1],
                                         scale=-1.0, accum_out=hsum[:, i, h:h + 1]).then_inc(s_prob, 1)

            def weights(t, h):
                s = t - 2
                act.wait_ge(s_pt, NH * s + h + 1)
                wait(act, s_pv, NH * s + max(h - 1, 0))
                nc.scalar.activation(pT_hi[:, h % 2, :, :].rearrange("p j i -> p (j i)"), bank_p[:, :], ACT.Copy).then_inc(s_pt_hi, 1)

            steps = {
                "split": split, "turn_x": turn_x, "turn_h": turn_h, "turn_y": turn_y,
                "a_scores": lambda t, k: graph_exp(layer_a(t)), "b_scores": lambda t, k: graph_exp(layer_b(t)),
                "a_proj": lambda t, k: proj_hi(layer_a(t), k), "b_proj": lambda t, k: proj_hi(layer_b(t), k),
                "a_turn": lambda t, k: graph_turn(layer_a(t)), "b_turn": lambda t, k: graph_turn(layer_b(t)),
                "h_norm": lambda t, k: root("a", t - 1), "b_norm": lambda t, k: root("b", t - 1),
                "b_norm2": lambda t, k: root("y", t - 1), "b_apply": b_apply, "c_norm": c_norm, "c_store": c_store,
                "q": lambda t, k: qk(t, 0, k), "k": lambda t, k: qk(t, 1, k), "v": v, "scores": scores, "weights": weights, "late_weights": lambda t, k: weights(t - 1, k),
            }
            pipeline(act, "act", lambda t, todo: run(steps, todo, t))

        @block.vector
        def _(dve):
            ve = nc.vector
            links = [0, 0]

            def mark(ins):
                ins.then_inc(s_dve, 1)
                links[1] += 1

            def settle():
                dve.wait_ge(s_dve, links[0] + links[1])

            def link(ins):
                mark(ins)
                settle()

            def constants():
                dve.wait_ge(s_pool_c, 6)
                for e, col in eps_col.items():
                    link(ve.memset(col[:, :], e))
                for l in range(LAYERS):
                    link(ve.tensor_tensor(pick_bias[l][:, :], ident[:, l:l + 1].to_broadcast([P, P]),
                                          ident[:, 32 + l:33 + l].to_broadcast([P, P]), ALU.add))
                dve.wait_ge(s_const, 16 * 14)
                for m, src in ((slice(0, 2), self_part[:, 0:2, :]), (slice(2, 3), mixed[:, 0:1, :])):
                    link(ve.tensor_copy(bias_rows[0:LAYERS, m, :], src[0:LAYERS]))
                    link(ve.tensor_copy(bias_rows[32:32 + LAYERS, m, :], src[32:32 + LAYERS]))
                    link(ve.tensor_tensor(bias_rows[32:32 + LAYERS, m, :], src[32:32 + LAYERS],
                                          bias_rows[32:32 + LAYERS, m, :], ALU.subtract))
                link(ve.tensor_scalar(beta_col[:, :], beta_col[:, :], 1.0 / SCALE, None, ALU.mult))

            def split(_t, n):
                if n == 0:
                    constants()
                w = (w_graph[0], w_graph[1], w_qkv)[n]
                for k in range(BATCH):
                    dve.wait_ge(s_w_hi, BATCH * n + k + 1)
                    ve.tensor_tensor(w[1][:, k % NC, k // NC, :], staging[(BATCH * n + k) % len(staging)],
                                     w[0][:, k % NC, k // NC, :], ALU.subtract).then_inc(s_split, 1)
                dve.wait_ge(s_split, BATCH * (n + 1))
                dve.sem_inc(s_setup, 1)

            def turn_x(t, k):
                dve.wait_ge(s_tx_hi, NC * t + k + 1)
                ve.tensor_tensor(hT_ac[1][:, k, :], bank_t[:, 0:S], hT_ac[0][:, k, :], ALU.subtract).then_inc(s_tx_lo, 1)

            def turn_y(t, k):
                dve.wait_ge(s_ty_hi, NC * (t - 1) + k + 1)
                ve.tensor_tensor(hT_ac[1][:, k, :], bank_t[:, 0:S], hT_ac[0][:, k, :], ALU.subtract).then_inc(s_ty_lo, 1)

            def turn_h(t, k):
                dve.wait_ge(s_th_f, 2 * (NC * (t - 1) + k + 1))
                f = mixed[:, 0, 0:S] if k == 0 else (mixed[:, 1, 0:S] if k == 1 else self_part[:, 0, 0:S])
                ve.tensor_tensor(hT_b[1][:, k, :], f, hT_b[0][:, k, :], ALU.subtract).then_inc(s_th_lo, 1)

            def graph_scores(n):
                dve.wait_ge(s_u, n + 1)
                link(ve.tensor_reduce(negmax[:, :], bank_u[:, :].rearrange("p (i j) -> p i j", i=NT), AX.X, ALU.max, negate=True))
                ve.tensor_scalar(ubias[:, :], negmax[:, :], TEMPER, None, ALU.mult).then_inc(s_ub, 1)

            def graph_mask(n, k, count):
                wait(dve, s_self, 2 * n)
                dve.wait_ge(s_adj[k], count)
                for i in range(NT):
                    dve.wait_ge(s_exp, 2 * n + i + 1)
                    ve.scalar_tensor_tensor(expu[:, i, :], expu[:, i, :], 1.0, adj_in[:, i, :], ALU.mult, ALU.mult,
                                            accum_out=ssum[:, i:i + 1]).then_inc(s_em, 1)
                dve.wait_ge(s_em, 2 * (n + 1))
                mark(ve.scalar_tensor_tensor(inv_s[k][:, :], zsum[:, :], EPS_ATTN, ssum[:, :], ALU.mult, ALU.add))
                for i in range(NT):
                    ve.scalar_tensor_tensor(diag_tmp[:, i, :], expu[:, i, i * P:(i + 1) * P], 1.0, ident[:, :],
                                            ALU.mult, ALU.mult, accum_out=diag[:, i:i + 1]).then_inc(s_diag, 1)
                settle()
                link(ve.reciprocal(inv_s[k][:, :], inv_s[k][:, :]))
                mark(ve.tensor_tensor(inv_s2[k][:, :], inv_s[k][:, :], inv_s[k][:, :], ALU.mult))

            def projection(n, j):
                m, i = j // 2, j % 2
                if m != 1:
                    dve.wait_ge(s_proj_hi, 4 * n + (j if m == 0 else j - 2) + 1)
                    ve.tensor_tensor(hlr[1][:, i, m // 2, :], bank_w[i][:, 0:D], hlr[0][:, i, m // 2, :],
                                     ALU.subtract).then_inc(s_proj_rd, 1)

            def graph_turn(n):
                dve.wait_ge(s_at_hi, n + 1)
                ve.tensor_tensor(attT[1][:, :, :].rearrange("p j i -> p (j i)"), bank_u[:, :],
                                 attT[0][:, :, :].rearrange("p j i -> p (j i)"), ALU.subtract).then_inc(s_at_lo, 1)

            def mix(n, i, k):
                dve.wait_ge(s_mix, 2 * n + i + 1)
                dve.wait_ge(s_self, 2 * (n + 1))
                ve.tensor_tensor(mixed[:, i, :], bank_m[:, 0:D], self_part[:, i, :], ALU.add).then_inc(s_mix_rd, 1)
                dve.wait_ge(s_mix_rd, 2 * n + i + 1)
                mark(ve.bn_stats(stats[k][:, i, :], mixed[:, i, :]))

            def refine(k, index, factor=None):
                v = var[k] if k in "yc" else var[k][:, :]
                y, t1, t2 = y0[k][:, :], tmp[k][:, :], rstd[k][:, :]
                dve.wait_ge(s_y0[k], index + 1)
                mark(ve.scalar_tensor_tensor(t1, v, eps[k], y, ALU.add, ALU.mult))
                if factor is not None:
                    mark(ve.tensor_tensor(t2, y, factor, ALU.mult))
                settle()
                link(ve.scalar_tensor_tensor(t1, t1, -0.5, y, ALU.mult, ALU.mult))
                link(ve.scalar_tensor_tensor(t2, t1, 1.5, y if factor is None else t2, ALU.add, ALU.mult))

            def graph_norm(k):
                settle()
                apart(dve)
                for i in range(NT):
                    mark(ve.bn_aggr(mv[k][:, i, :], stats[k][:, i, :]))
                settle()
                ve.tensor_tensor(var[k][:, :], mv[k][:, :, 1], inv_s2[k][:, :], ALU.mult).then_inc(s_var[k], 1)

            def h_apply(t, _k):
                refine("a", t - 1, inv_s["a"][:, :])
                for i in range(NT):
                    ve.tensor_scalar(normed[:, i, :], mixed[:, i, :], mv["a"][:, i, 0:1], rstd["a"][:, i:i + 1],
                                     ALU.subtract, ALU.mult).then_inc(s_h1, 1)

            def b_apply(t, _k):
                refine("b", t - 1, inv_s["b"][:, :])
                ve.scalar_tensor_tensor(shift[:, :], mv["b"][:, :, 0], -1.0, rstd["b"][:, :], ALU.mult, ALU.mult
                                        ).then_inc(s_shift, 1)

            def b_resid(t, i):
                if i == 0:
                    dve.wait_ge(s_xb, 16 * t)
                dve.wait_ge(s_affine, NT * (t - 1) + i + 1)
                ve.scalar_tensor_tensor(normed[:, i, :], normed[:, i, :], 0.0, x_in[:, i, :],
                                        ALU.max, ALU.add).then_inc(s_resid, 1)
                dve.wait_ge(s_resid, NT * (t - 1) + i + 1)
                mark(ve.bn_stats(stats["y"][:, i, :], normed[:, i, :]))

            def b_norm2(t, _k):
                settle()
                apart(dve)
                for i in range(NT):
                    ve.bn_aggr(mv["y"][:, i, :], stats["y"][:, i, :]).then_inc(s_var["y"], 1)

            def b_out(t, _k):
                refine("y", t - 1)
                if not (isinstance(t, int) and t == 1):
                    dve.wait_ge(s_res, t - 1)
                for i in range(NT):
                    ve.tensor_scalar(y_in[:, i, :], normed[:, i, :], mv["y"][:, i, 0:1], rstd["y"][:, i:i + 1],
                                     ALU.subtract, ALU.mult).then_inc(s_y, 1)

            def qk(t, side, g):
                s, j = t - 2, NC * side + g
                dve.wait_ge(s_qk_hi, 6 * s + j + 1)
                ve.scalar_tensor_tensor(qk_lo[:, side, g, :], bank_w[j % 2][:, 0:S],
                                        (q_bias, k_bias)[side][:, g:g + 1], qk_hi[:, side, g, :],
                                        ALU.add, ALU.subtract).then_inc(s_qk_lo, 1)

            def v(t, i):
                s = t - 2
                dve.wait_ge(s_v_hi, NT * s + i + 1)
                if i == 0:
                    dve.wait_ge(s_badj, s + 1)
                ve.tensor_tensor(v_rest[:, i, :].rearrange("p (h d) -> p h d", h=NH),
                                 bank_w[i][:, 0:D].rearrange("p (h d) -> p h d", h=NH),
                                 v_parts[:, i, :, 0, :], ALU.subtract).then_inc(s_v_rd, 1)

            def scores(t, h):
                s = t - 2
                dve.wait_ge(s_sc, NH * s + h + 1)
                if h == 0:
                    dve.wait_ge(s_badj, s + 1)
                wait(dve, s_prob, NT * (NH * s + h))
                apart(dve)
                for i in range(NT):
                    ve.tensor_tensor_reduce(masked[:, i, :], bank_s[:, i * S:(i + 1) * S], bias_adj[:, i, :],
                                            -SCALE, BIG, ALU.add, ALU.min, hmin[:, i, h:h + 1]).then_inc(s_msk, 1)

            def weights(t, h):
                s = t - 2
                dve.wait_ge(s_pt_hi, NH * s + h + 1)
                ve.tensor_tensor(pT_lo[:, h % 2, :, :].rearrange("p j i -> p (j i)"), bank_p[:, :],
                                 pT_hi[:, h % 2, :, :].rearrange("p j i -> p (j i)"), ALU.subtract).then_inc(s_pt_lo, 1)

            def attend(t, h):
                if h % 2 == 1:
                    s = t - 2
                    if h == 1:
                        wait(dve, s_out, 16 * s)
                    dve.wait_ge(s_pv, NH * s + h + 1)
                    ve.tensor_reduce(att[:, :, h - 1:h + 1, :],
                                     bank_o[:, 0:NT * 2 * VP * HD].rearrange("p (i h a d) -> p i h d a", i=NT, h=2, a=VP),
                                     AX.X, ALU.add).then_inc(s_att, 1)

            def c_sum(t, _k):
                s = t - 3
                dve.wait_ge(s_prob, NT * NH * (s + 1))
                ve.reciprocal(hinv[:, :, :], hsum[:, :, :]).then_inc(s_hinv, 1)

            def c_stat(t, i):
                dve.wait_ge(s_csum, NT * (t - 3) + i + 1)
                mark(ve.bn_stats(stats["c"][:, i, :], result[:, i, :]))

            def c_norm(t, _k):
                settle()
                apart(dve)
                for i in range(NT):
                    ve.bn_aggr(mv["c"][:, i, :], stats["c"][:, i, :]).then_inc(s_var["c"], 1)

            def c_apply(t, _k):
                refine("c", t - 3)
                for i in range(NT):
                    ve.tensor_scalar(result[:, i, :], result[:, i, :], mv["c"][:, i, 0:1], rstd["c"][:, i:i + 1],
                                     ALU.subtract, ALU.mult).then_inc(s_out_ok, 1)

            def a_mask(t, _k):
                graph_mask(layer_a(t), "a", 16 * (t + 1))

            def b_mask(t, _k):
                graph_mask(layer_b(t), "b", 16 * t)

            steps = {
                "split": split, "turn_x": turn_x, "turn_h": turn_h, "turn_y": turn_y,
                "a_scores": lambda t, k: graph_scores(layer_a(t)), "b_scores": lambda t, k: graph_scores(layer_b(t)),
                "a_mask": a_mask, "b_mask": b_mask,
                "a_proj": lambda t, k: projection(layer_a(t), k), "b_proj": lambda t, k: projection(layer_b(t), k),
                "a_turn": lambda t, k: graph_turn(layer_a(t)), "b_turn": lambda t, k: graph_turn(layer_b(t)),
                "a_mix": lambda t, k: mix(layer_a(t), k, "a"), "b_mix": lambda t, k: mix(layer_b(t), k, "b"),
                "h_norm": lambda t, k: graph_norm("a"), "b_norm": lambda t, k: graph_norm("b"),
                "h_apply": h_apply, "b_apply": b_apply, "b_resid": b_resid,
                "b_norm2": b_norm2, "b_out": b_out, "c_sum": c_sum, "c_stat": c_stat, "c_norm": c_norm, "c_apply": c_apply,
                "q": lambda t, k: qk(t, 0, k), "k": lambda t, k: qk(t, 1, k), "v": v, "scores": scores, "weights": weights, "late_weights": lambda t, k: weights(t - 1, k), "attend": attend,
                "late_attend": lambda t, k: attend(t - 1, k),
            }
            PER_ITERATION = 34

            def body(t, todo):
                if not isinstance(t, int):
                    links[0] = links[0] + links[1] + (t - 3) * PER_ITERATION
                    links[1] = 0
                run(steps, todo, t)
                if not isinstance(t, int):
                    assert links[1] == PER_ITERATION, links[1]
                    links[0], links[1] = base[0] + (NB - 3) * PER_ITERATION, 0
                else:
                    links[0], links[1] = links[0] + links[1], 0
                    base[0] = links[0]

            base = [0]
            pipeline(dve, "dve", body)

        @block.gpsimd
        def _(pool):
            gp = nc.gpsimd
            gp.memset(bias_rows[:, :, :].bitcast(F32), 0.0).then_inc(s_pool_c, 1)
            gp.memset(ident[:, :], 1.0).then_inc(s_pool_c, 1)
            gp.memset(mask_up[:, :], 1.0).then_inc(s_pool_c, 1)
            pool.wait_ge(s_pool_c, 3)
            gp.affine_select(out=ident[:, :], in_=ident[:, :], pattern=[[-1, P]], compare_op=ALU.is_equal, fill=0.0,
                             base=0, channel_multiplier=1).then_inc(s_pool_c, 1)
            gp.affine_select(out=mask_low[:, :], in_=mask_up[:, :], pattern=[[1, P]], compare_op=ALU.is_gt, fill=0.0,
                             base=0, channel_multiplier=-1).then_inc(s_pool_c, 1)
            pool.wait_ge(s_pool_c, 5)
            gp.affine_select(out=mask_up[:, :], in_=mask_up[:, :], pattern=[[-1, P]], compare_op=ALU.is_gt, fill=0.0,
                             base=0, channel_multiplier=1).then_inc(s_pool_c, 1)
            pool.wait_ge(s_pool_c, 6)
            pool.wait_ge(s_setup, 1)

            def graph_turn(n):
                pool.wait_ge(s_at_lo, n + 1)
                wait(pool, s_mix, 2 * n)
                for part in range(2):
                    blocks = attT[part][:, :, :].rearrange("p j (i q) -> p (j i) q", i=NT)[:, 0::3, :]
                    for dst, keep in ((up, mask_up), (low, mask_low)):
                        ins = gp.tensor_tensor(dst[part][:, :, :], blocks,
                                               keep[:, :].unsqueeze(1).to_broadcast([P, NT, P]), ALU.mult)
                ins.then_inc(s_cut, 1)

            def q(t, g):
                s = t - 2
                if g == 0:
                    pool.wait_ge(s_adj["c"], 16 * (s + 1))
                    wait(pool, s_msk, NT * NH * s)
                    wait(pool, s_v_all, NT * s)
                    apart(pool)
                    gp.tensor_scalar(neg_adj[:, :, :], adj_in[:, :, :], 0.0, MASKED / SCALE, ALU.is_le, ALU.mult
                                     ).then_inc(s_pool, 1)
                    gp.tensor_scalar(bias_adj[:, :, :], adj_in[:, :, :], 0.0, beta_col[:, 0:1], ALU.max, ALU.mult
                                     ).then_inc(s_pool, 1)
                    pool.wait_ge(s_pool, 2 * (s + 1))
                    gp.tensor_tensor(bias_adj[:, :, :], bias_adj[:, :, :], neg_adj[:, :, :], ALU.add).then_inc(s_badj, 1)
                if g == 2:
                    pool.wait_ge(s_y, NT * (s + 1))
                    wait(pool, s_csum, NT * s)
                    gp.tensor_tensor(res[:, :, :], y_in[:, :, :], v_bias[:, :].unsqueeze(1).to_broadcast([P, NT, D]),
                                     ALU.add).then_inc(s_res, 1)

            def b_apply(t, _k):
                s = t - 1
                for i in range(NT):
                    pool.wait_ge(s_scaled, NT * s + i + 1)
                    gp.tensor_tensor(normed[:, i, :], normed[:, i, :], g2_row[:, :], ALU.mult).then_inc(s_affine_mid, 1)
                for i in range(NT):
                    pool.wait_ge(s_affine_mid, NT * s + i + 1)
                    gp.tensor_tensor(normed[:, i, :], normed[:, i, :], b2_row[:, :], ALU.add).then_inc(s_affine, 1)

            def c_sum(t, _k):
                s = t - 3
                pool.wait_ge(s_hinv, s + 1)
                pool.wait_ge(s_att, NH // 2 * (s + 1))
                for i in range(NT):
                    gp.tensor_tensor(att[:, i, :, :], att[:, i, :, :],
                                     hinv[:, i, :].unsqueeze(2).to_broadcast([P, NH, HD]), ALU.mult).then_inc(s_csum_mid, 1)
                for i in range(NT):
                    pool.wait_ge(s_csum_mid, NT * s + i + 1)
                    gp.tensor_tensor(result[:, i, :], result[:, i, :], res[:, i, :], ALU.add).then_inc(s_csum, 1)

            def v(t, i):
                s = t - 2
                pool.wait_ge(s_v_rd, NT * s + i + 1)
                wait(pool, s_pv, NH * s)
                apart(pool)
                rest = v_rest[:, i, :].rearrange("p (h d) -> p h d", h=NH)
                gp.tensor_copy(v_parts[:, i, :, 1, :], rest).then_inc(s_v_mid, 1)
                pool.wait_ge(s_v_mid, NT * s + i + 1)
                gp.tensor_tensor(v_parts[:, i, :, 2, :], rest, v_parts[:, i, :, 1, :], ALU.subtract).then_inc(s_v_all, 1)

            steps = {
                "a_turn": lambda t, k: graph_turn(layer_a(t)), "b_turn": lambda t, k: graph_turn(layer_b(t)),
                "q": q, "v": v, "b_apply": b_apply, "c_sum": c_sum,
                "split": lambda t, n: pool.wait_ge(s_setup, n + 1),
            }
            pipeline(pool, "pool", lambda t, todo: run(steps, todo, t))


_WEIGHTS_T = ("L0_gnn_Wl", "L0_gnn_Ws", "L0_gnn_Wr")
_INS = ["x", "adj", "L0_gnn_Wl", "L0_gnn_Ws", "L0_gnn_Wr", "L0_gnn_bl", "L0_gnn_bs", "L0_gnn_br",
        "L0_gnn_ln_w", "L0_gnn_ln_b", "L1_gnn_Wq", "L1_gnn_Wk", "L1_gnn_Wv", "L1_gnn_bq", "L1_gnn_bk",
        "L1_gnn_bv", "L1_gnn_beta"]


def kernel(**inputs):
    import concourse.bacc as _bacc
    from concourse.bass_utils import run_bass_kernel_spmd as _run

    nc = _bacc.Bacc("TRN2", target_bir_lowering=False, num_devices=1)
    arrays, args = {}, []
    for name in _INS:
        a = np.asarray(inputs[name])
        if name in _WEIGHTS_T:
            a = a.transpose(0, 2, 1)
        if a.ndim == 0:
            a = a.reshape(1)
        a = np.ascontiguousarray(a)
        arrays[f"in_{name}"] = a
        args.append(nc.dram_tensor(f"in_{name}", a.shape, mybir.dt.from_np(a.dtype), kind="ExternalInput").ap())
    shape = arrays["in_x"].shape
    args.append(nc.dram_tensor("out_0", shape, F32, kind="ExternalOutput").ap())
    graph_attention_kernel(nc, *args)
    r = _run(nc, [arrays], core_ids=[0])
    return r.results[0]["out_0"]
```
